# Optimizing a Trainium2 kernel written in Bass

```python
import numpy as np
import jax
import jax.numpy as jnp

def _softmax(x, axis=-1):
    return jax.nn.softmax(x, axis=axis)

def _gelu(x):
    return jax.nn.gelu(x, approximate=True)

def _silu(x):
    return jax.nn.silu(x)

def _sigmoid(x):
    return jax.nn.sigmoid(x)

def _layernorm(x, axis=-1, eps=1e-05):
    m = jnp.mean(x, axis=axis, keepdims=True)
    v = jnp.var(x, axis=axis, keepdims=True)
    return (x - m) / jnp.sqrt(v + eps)

def _scatter_add(tgt, idx, src, axis=0):
    return tgt.at[idx].add(src)

def _segment_sum(src, seg, n):
    return jax.ops.segment_sum(src, seg, n)
kernel_name = 'mk_decoder_postln_d1_seqx_r8_98181a'

def setup_inputs(seed: int=0):
    np.random.seed(seed)
    _w = jnp.asarray

    def _rec_inputs():
        import jax
        import jax.numpy as jnp
        _rk = jax.random.key(seed)
        x = -0.0002928 + 1 * jax.random.normal(jax.random.fold_in(_rk, 1), (16, 128, 128), jnp.float32)
        _lenS = 128 - jax.random.randint(jax.random.fold_in(_rk, 7), (16,), 0, max(1, 128 // 4) + 1, jnp.int32)
        _lenS2 = 128 - jax.random.randint(jax.random.fold_in(_rk, 8), (16,), 0, max(1, 128 // 4) + 1, jnp.int32)
        _ctx_1024P = jax.random.normal(jax.random.fold_in(_rk, 11), (16, 16, 128), jnp.float32)
        _ctx_1024c = jax.random.dirichlet(jax.random.fold_in(_rk, 511), 0.3 * jnp.ones((16,), jnp.float32), (16, 128))
        _ctx_1024t = jnp.einsum('bsk,bkd->bsd', _ctx_1024c, _ctx_1024P)
        _ctx_1024t = _ctx_1024t * jax.lax.rsqrt(jnp.mean(jnp.square(_ctx_1024t)) + 1e-12) * 0.953939
        ctx_1024 = -1.39393e-06 + 0.999914 * (_ctx_1024t + 0.3 * jax.random.normal(jax.random.fold_in(_rk, 611), (16, 128, 128), jnp.float32))
        return (x, ctx_1024)
    x, ctx_1024 = _rec_inputs()

    def _L0_attn_setup():
        import jax, jax.numpy as jnp
        import numpy as np
        E = 128
        H = 16
        HD = E // H
        MAX_REL = 20
        key = jax.random.key(seed)
        ks = jax.random.split(key, 12)
        B, S = (4, 128)

        def lin_w(k):
            return jax.random.normal(k, (E, E), dtype=jnp.float32) * (1.0 / np.sqrt(E))
        return {'hidden_states': jax.random.normal(ks[0], (B, S, E), dtype=jnp.float32), 'Wq': lin_w(ks[1]), 'bq': jnp.zeros((E,), jnp.float32), 'Wk': lin_w(ks[2]), 'bk': jnp.zeros((E,), jnp.float32), 'Wv': lin_w(ks[3]), 'bv': jnp.zeros((E,), jnp.float32), 'Wo': lin_w(ks[4]), 'bo': jnp.zeros((E,), jnp.float32), 'rel_k': jax.random.uniform(ks[5], (2 * MAX_REL + 1, HD), jnp.float32, -0.24, 0.24), 'rel_v': jax.random.uniform(ks[6], (2 * MAX_REL + 1, HD), jnp.float32, -0.24, 0.24)}
    _L0_attn_all = _L0_attn_setup()
    _L0_attn_in = {k: v for k, v in _L0_attn_all.items() if k in ('Wq', 'bq', 'Wk', 'bk', 'Wv', 'bv', 'Wo', 'bo', 'rel_k', 'rel_v')}
    del _L0_attn_all

    def _L0_xattn_setup():
        import jax, jax.numpy as jnp
        import numpy as np
        B, T, D_MODEL, N_HEAD = (1, 512, 128, 16)
        HEAD_DIM = D_MODEL // N_HEAD
        IS_CAUSAL = True

        def _mha(querys, keys, values, Wq, bq, Wk, bk, Wv, bv, Wo, bo):
            b, t, c = querys.shape
            q = (querys @ Wq.T + bq).reshape(b, t, N_HEAD, HEAD_DIM).transpose(0, 2, 1, 3)
            k = (keys @ Wk.T + bk).reshape(b, t, N_HEAD, HEAD_DIM).transpose(0, 2, 1, 3)
            v = (values @ Wv.T + bv).reshape(b, t, N_HEAD, HEAD_DIM).transpose(0, 2, 1, 3)
            scores = jnp.einsum('bhqd,bhkd->bhqk', q, k) / jnp.sqrt(jnp.float32(HEAD_DIM))
            if IS_CAUSAL:
                causal = jnp.tril(jnp.ones((t, t), dtype=bool))
                scores = jnp.where(causal, scores, jnp.float32(-jnp.inf))
            weights = jax.nn.softmax(scores, axis=-1)
            attn = jnp.einsum('bhqk,bhkd->bhqd', weights, v)
            out = attn.transpose(0, 2, 1, 3).reshape(b, t, c)
            return out @ Wo.T + bo
        key = jax.random.key(seed)
        ks = jax.random.split(key, 11)
        s_in = 1.0 / np.sqrt(D_MODEL)
        return {'querys': jax.random.normal(ks[0], (B, T, D_MODEL), dtype=jnp.float32), 'keys': jax.random.normal(ks[1], (B, T, D_MODEL), dtype=jnp.float32), 'values': jax.random.normal(ks[2], (B, T, D_MODEL), dtype=jnp.float32), 'Wq': jax.random.normal(ks[3], (D_MODEL, D_MODEL), dtype=jnp.float32) * s_in, 'bq': jnp.zeros((D_MODEL,), dtype=jnp.float32), 'Wk': jax.random.normal(ks[4], (D_MODEL, D_MODEL), dtype=jnp.float32) * s_in, 'bk': jnp.zeros((D_MODEL,), dtype=jnp.float32), 'Wv': jax.random.normal(ks[5], (D_MODEL, D_MODEL), dtype=jnp.float32) * s_in, 'bv': jnpp_zeros() if False else jnp.zeros((D_MODEL,), dtype=jnp.float32), 'Wo': jax.random.normal(ks[6], (D_MODEL, D_MODEL), dtype=jnp.float32) * s_in, 'bo': jnp.zeros((D_MODEL,), dtype=jnp.float32)}
    _L0_xattn_all = _L0_xattn_setup()
    _L0_xattn_in = {k: v for k, v in _L0_xattn_all.items() if k in ('Wq', 'bq', 'Wk', 'bk', 'Wv', 'bv', 'Wo', 'bo')}
    del _L0_xattn_all

    def _L0_ffn_setup():
        import jax, jax.numpy as jnp
        import numpy as np
        D = 128
        H = 256
        E = 8
        TOP_K = 2
        N_SHARED = 1
        B, S = (2, 128)
        key = jax.random.key(seed)
        ks = jax.random.split(key, 12)
        sc = 0.02
        return {'hidden': jax.random.normal(ks[0], (B, S, D), jnp.float32), 'router_w': jax.random.normal(ks[1], (D, E), jnp.float32) * sc, 'router_b': jnp.zeros((E,), jnp.float32), 'sw1': jax.random.normal(ks[2], (D, H), jnp.float32) * sc, 'sb1': jnp.zeros((H,), jnp.float32), 'sw2': jax.random.normal(ks[3], (H, D), jnp.float32) * sc, 'sb2': jnp.zeros((D,), jnp.float32), 'rw1': jax.random.normal(ks[4], (E, D, H), jnp.float32) * sc, 'rb1': jnp.zeros((E, H), jnp.float32), 'rw2': jax.random.normal(ks[5], (E, H, D), jnp.float32) * sc, 'rb2': jnp.zeros((E, D), jnp.float32)}
    _L0_ffn_all = _L0_ffn_setup()
    _L0_ffn_in = {k: v for k, v in _L0_ffn_all.items() if k in ('router_w', 'router_b', 'sw1', 'sb1', 'sw2', 'sb2', 'rw1', 'rb1', 'rw2', 'rb2')}
    del _L0_ffn_all
    return {'x': x, 'ctx_1024': ctx_1024, 'L0_attn_Wq': _L0_attn_in['Wq'], 'L0_attn_bq': _L0_attn_in['bq'], 'L0_attn_Wk': _L0_attn_in['Wk'], 'L0_attn_bk': _L0_attn_in['bk'], 'L0_attn_Wv': _L0_attn_in['Wv'], 'L0_attn_bv': _L0_attn_in['bv'], 'L0_attn_Wo': _L0_attn_in['Wo'], 'L0_attn_bo': _L0_attn_in['bo'], 'L0_attn_rel_k': _L0_attn_in['rel_k'], 'L0_attn_rel_v': _L0_attn_in['rel_v'], 'L0_xattn_Wq': _L0_xattn_in['Wq'], 'L0_xattn_bq': _L0_xattn_in['bq'], 'L0_xattn_Wk': _L0_xattn_in['Wk'], 'L0_xattn_bk': _L0_xattn_in['bk'], 'L0_xattn_Wv': _L0_xattn_in['Wv'], 'L0_xattn_bv': _L0_xattn_in['bv'], 'L0_xattn_Wo': _L0_xattn_in['Wo'], 'L0_xattn_bo': _L0_xattn_in['bo'], 'L0_ffn_router_w': _L0_ffn_in['router_w'], 'L0_ffn_router_b': _L0_ffn_in['router_b'], 'L0_ffn_sw1': _L0_ffn_in['sw1'], 'L0_ffn_sb1': _L0_ffn_in['sb1'], 'L0_ffn_sw2': _L0_ffn_in['sw2'], 'L0_ffn_sb2': _L0_ffn_in['sb2'], 'L0_ffn_rw1': _L0_ffn_in['rw1'], 'L0_ffn_rb1': _L0_ffn_in['rb1'], 'L0_ffn_rw2': _L0_ffn_in['rw2'], 'L0_ffn_rb2': _L0_ffn_in['rb2']}

def reference(x, ctx_1024, L0_attn_Wq, L0_attn_bq, L0_attn_Wk, L0_attn_bk, L0_attn_Wv, L0_attn_bv, L0_attn_Wo, L0_attn_bo, L0_attn_rel_k, L0_attn_rel_v, L0_xattn_Wq, L0_xattn_bq, L0_xattn_Wk, L0_xattn_bk, L0_xattn_Wv, L0_xattn_bv, L0_xattn_Wo, L0_xattn_bo, L0_ffn_router_w, L0_ffn_router_b, L0_ffn_sw1, L0_ffn_sb1, L0_ffn_sw2, L0_ffn_sb2, L0_ffn_rw1, L0_ffn_rb1, L0_ffn_rw2, L0_ffn_rb2):
    import jax
    import jax.numpy as jnp

    def _L0_attn_ref(hidden_states, Wq, bq, Wk, bk, Wv, bv, Wo, bo, rel_k, rel_v):
        import jax, jax.numpy as jnp
        import numpy as np
        E = 128
        H = 16
        HD = E // H
        MAX_REL = 20
        B, S, _ = hidden_states.shape
        scale = jnp.sqrt(jnp.float32(HD))

        def proj(W, b):
            return (hidden_states @ W.T + b).reshape(B, S, H, HD).transpose(0, 2, 1, 3)
        q = proj(Wq, bq)
        k = proj(Wk, bk)
        v = proj(Wv, bv)
        pos = jnp.arange(S)
        idx = jnp.clip(pos[None, :] - pos[:, None], -MAX_REL, MAX_REL) + MAX_REL
        rk2 = rel_k[idx]
        rv2 = rel_v[idx]
        attn1 = jnp.einsum('bhqd,bhkd->bhqk', q, k)
        attn2 = jnp.einsum('bhqd,qkd->bhqk', q, rk2)
        attn = jax.nn.softmax((attn1 + attn2) / scale, axis=-1)
        w1 = jnp.einsum('bhqk,bhkd->bhqd', attn, v)
        w2 = jnp.einsum('bhqk,qkd->bhqd', attn, rv2)
        x = (w1 + w2).transpose(0, 2, 1, 3).reshape(B, S, E)
        out = x @ Wo.T + bo
        return out

    def _L0_xattn_ref(querys, keys, values, Wq, bq, Wk, bk, Wv, bv, Wo, bo):
        import jax, jax.numpy as jnp
        import numpy as np
        B, T, D_MODEL, N_HEAD = (1, 512, 128, 16)
        HEAD_DIM = D_MODEL // N_HEAD
        IS_CAUSAL = True

        def _mha(querys, keys, values, Wq, bq, Wk, bk, Wv, bv, Wo, bo):
            b, t, c = querys.shape
            q = (querys @ Wq.T + bq).reshape(b, t, N_HEAD, HEAD_DIM).transpose(0, 2, 1, 3)
            k = (keys @ Wk.T + bk).reshape(b, t, N_HEAD, HEAD_DIM).transpose(0, 2, 1, 3)
            v = (values @ Wv.T + bv).reshape(b, t, N_HEAD, HEAD_DIM).transpose(0, 2, 1, 3)
            scores = jnp.einsum('bhqd,bhkd->bhqk', q, k) / jnp.sqrt(jnp.float32(HEAD_DIM))
            if IS_CAUSAL:
                causal = jnp.tril(jnp.ones((t, t), dtype=bool))
                scores = jnp.where(causal, scores, jnp.float32(-jnp.inf))
            weights = jax.nn.softmax(scores, axis=-1)
            attn = jnp.einsum('bhqk,bhkd->bhqd', weights, v)
            out = attn.transpose(0, 2, 1, 3).reshape(b, t, c)
            return out @ Wo.T + bo
        return _mha(querys, keys, values, Wq, bq, Wk, bk, Wv, bv, Wo, bo)

    def _L0_ffn_ref(hidden, router_w, router_b, sw1, sb1, sw2, sb2, rw1, rb1, rw2, rb2):
        import jax, jax.numpy as jnp
        import numpy as np
        D = 128
        H = 256
        E = 8
        TOP_K = 2
        N_SHARED = 1
        B, S = (2, 128)
        b, s, d = hidden.shape
        T = b * s
        flat = hidden.reshape(T, d)
        router_logits = flat @ router_w + router_b
        router_probs = jax.nn.softmax(router_logits, axis=-1)
        topk_probs, topk_idx = jax.lax.top_k(router_probs, TOP_K)
        weights = jnp.zeros_like(router_probs).at[jnp.arange(T)[:, None], topk_idx].add(topk_probs)
        sh = jax.nn.gelu(flat @ sw1 + sb1, approximate=False)
        shared_out = (sh @ sw2 + sb2) / N_SHARED
        h1 = jax.nn.gelu(jnp.einsum('td,edh->teh', flat, rw1) + rb1[None], approximate=False)
        expert_out = jnp.einsum('teh,ehd->ted', h1, rw2) + rb2[None]
        mixed = jnp.einsum('ted,te->td', expert_out, weights)
        return (shared_out + mixed).reshape(b, s, d)
    x = _layernorm(x + _L0_attn_ref(x, L0_attn_Wq, L0_attn_bq, L0_attn_Wk, L0_attn_bk, L0_attn_Wv, L0_attn_bv, L0_attn_Wo, L0_attn_bo, L0_attn_rel_k, L0_attn_rel_v), axis=-1)
    x = _layernorm(x + _L0_xattn_ref(x, ctx_1024, ctx_1024, L0_xattn_Wq, L0_xattn_bq, L0_xattn_Wk, L0_xattn_bk, L0_xattn_Wv, L0_xattn_bv, L0_xattn_Wo, L0_xattn_bo), axis=-1)
    x = _layernorm(x + _L0_ffn_ref(x, L0_ffn_router_w, L0_ffn_router_b, L0_ffn_sw1, L0_ffn_sb1, L0_ffn_sw2, L0_ffn_sb2, L0_ffn_rw1, L0_ffn_rb1, L0_ffn_rw2, L0_ffn_rb2), axis=-1)
    return x

_drawn_inputs = setup_inputs


def setup_inputs(seed=0):
    import zlib

    import numpy as np

    out = dict(_drawn_inputs(seed))
    spreads = {'L0_attn_bq': (0.0, 0.582),
     'L0_attn_bk': (0.0, 0.8),
     'L0_attn_bv': (0.0, 0.1),
     'L0_attn_bo': (0.0, 0.1),
     'L0_xattn_bq': (0.0, 0.349),
     'L0_xattn_bk': (0.0, 0.8),
     'L0_xattn_bv': (0.0, 0.1),
     'L0_xattn_bo': (0.0, 0.1),
     'L0_ffn_router_b': (0.0, 0.627),
     'L0_ffn_sb1': (0.0, 0.515),
     'L0_ffn_sb2': (0.0, 0.1),
     'L0_ffn_rb1': (0.0, 0.8),
     'L0_ffn_rb2': (0.0, 0.348)}
    factors = {'L0_attn_rel_k': 2.769, 'L0_ffn_rw1': 6.62, 'L0_ffn_rw2': 5.906}
    for name, (base, spread) in spreads.items():
        noise = np.random.default_rng([zlib.crc32(name.encode()), seed]).standard_normal(out[name].shape)
        drawn = base * np.exp(spread * noise) if base else spread * noise
        out[name] = jnp.asarray(drawn.astype(out[name].dtype))
    for name, factor in factors.items():
        out[name] = (out[name] * factor).astype(out[name].dtype)
    return out
```

```python
import concourse.bass as bass
from concourse import mybir
from contextlib import ExitStack

F32 = mybir.dt.float32
BF16 = mybir.dt.bfloat16
ACT = mybir.ActivationFunctionType
ALU = mybir.AluOpType
AXIS = mybir.AxisListType

P = 128
S = 128
E = 128
H = 16
HD = E // H
MAX_REL = 20
NREL = 2 * MAX_REL + 1
NB = 4
T = NB * S
HB = H * NB
HB_TILE = 8
TILE = HB_TILE * S
NT = HB // HB_TILE
BANK = 512
NEXP = 8
TOP_K = 2
HID = 256
NF = HID // P
WIN = 2 * S - 1
WPAD = 256
EPS = 1e-5
SCALE = float(HD) ** -0.5
MASKED = -1.0e30
PAD = 32

Q_PART = [0, 0, 0, 1, 1, 2]
K_PART = [0, 1, 2, 0, 1, 0]
NC = len(Q_PART)
KD = NC * HD
NSH = 3
KD2 = KD + NSH


def build(nc, x, ctx, sw, cw, rel_k, rel_v, router_w, router_b, sw1, sb1, sw2, sb2,
          rw1, rb1, rw2, rb2, rel_ext, spread, out):
    n_seq = x.shape[0]
    NCH = n_seq // NB
    xv = x.rearrange("(c b) s e -> c s b e", b=NB)
    cv = ctx.rearrange("(c b) s e -> c s b e", b=NB)
    ov = out.rearrange("(c b) s e -> c s b e", b=NB)

    st = ExitStack()
    with st:
        def sb(name, shape, dt=F32):
            return st.enter_context(nc.sbuf_tensor(name, shape, dt))

        def sem(name):
            return st.enter_context(nc.semaphore(name))

        ident = sb("ident", [P, P])
        identb = sb("identb", [P, P], BF16)
        maskT = sb("maskT", [P, 4, S], BF16)
        wT = sb("wT", [P, 8, P])
        bcol = sb("bcol", [P, 4])
        brow = sb("brow", [P, 4, E])
        rb_row = sb("rb_row", [P, NEXP])
        hb = sb("hb", [P, NEXP + 1, NF])
        ob = sb("ob", [NEXP + 1, E])
        w1 = sb("w1", [P, NEXP + 1, HID])
        w2 = sb("w2", [P, NEXP + 1, NF, E])
        wr = sb("wr", [P, NEXP])
        tri = sb("tri", [P, NEXP, NEXP])
        epst = sb("epst", [P, NB])
        halfm = sb("halfm", [P, NB])
        relx = sb("relx", [HD, WPAD])
        relr = sb("relr", [HD, WPAD])
        relp = sb("relp", [HD, 3, WPAD], BF16)
        RK = sb("RK", [KD, WPAD], BF16)
        RV = sb("RV", [P, S, HD])

        xin = sb("xin", [P, NB, E])
        cin = sb("cin", [P, NB, E])
        xb = sb("xb", [P, NB, E])
        actT = sb("actT", [P, T])
        ctxT = sb("ctxT", [P, T])
        part = [sb(f"part{i}", [P, 3, T], BF16) for i in range(2)]
        rest = [sb(f"rest{i}", [P, T]) for i in range(2)]
        QS = [sb(f"QS{i}", [KD2, HB * S], BF16) for i in range(2)]
        KS = [sb(f"KS{i}", [KD2, HB * S], BF16) for i in range(2)]
        VA = [sb(f"VA{i}", [P, NB, H, PAD]) for i in range(2)]
        ST = sb("ST", [P, HB * S])
        SUM = sb("SUM", [P, 2, TILE])
        MX = sb("MX", [P, HB * 4])
        NM = sb("NM", [P, 2, 32])
        NR = sb("NR", [P, 2, 32])
        MP = sb("MP", [P, NSH, 2, 32], BF16)
        OT = sb("OT", [P, 2 * TILE])
        wnat = OT[:, 0:8 * P].rearrange("p (w i) -> p w i", w=8)
        rl = sb("rl", [P, 2, 8, NB])
        X = sb("X", [P, NB, H, HD])
        XT = sb("XT", [P, T])
        Y = sb("Y", [P, NB, E])
        stats = sb("stats", [P, NB, 6])
        mv = sb("mv", [P, NB, 2])
        ve = sb("ve", [P, NB])
        rstd = sb("rstd", [P, NB])
        x1 = sb("x1", [P, NB, E])
        lg = sb("lg", [P, NB, NEXP])
        lmax = sb("lmax", [P, NB])
        pe_ = sb("pe_", [P, NB, NEXP])
        lsum = sb("lsum", [P, NB])
        gt = sb("gt", [P, NB, NEXP, NEXP])
        eq = sb("eq", [P, NB, NEXP, NEXP])
        rank = sb("rank", [P, NB, NEXP])
        gw = sb("gw", [P, NB, PAD])
        gwT = sb("gwT", [NEXP + 1, NB, P])
        HT = [sb(f"HT{i}", [P, NF, T]) for i in range(2)]
        acc = Y

        ps_s = [st.enter_context(nc.psum_tensor(f"ps_s{i}", [P, TILE], F32)) for i in range(2)]
        ps_o = st.enter_context(nc.psum_tensor("ps_o", [P, TILE], F32))
        ps_f = [st.enter_context(nc.psum_tensor(f"ps_f{i}", [P, BANK], F32)) for i in range(2)]

        ld_w = sem("ld_w")
        ld_rel = sem("ld_rel")
        ext_done = sem("ext_done")
        ld_rk = sem("ld_rk")
        spread_out = sem("spread_out")
        ld_x = sem("ld_x")
        ld_c = sem("ld_c")
        c_pool = sem("c_pool")
        c_dve = sem("c_dve")
        rel_ready = sem("rel_ready")
        wt_ps = sem("wt_ps")
        wt_sb = sem("wt_sb")
        s_full = sem("s_full")
        s_free = [sem(f"s_free{i}") for i in range(2)]
        o_full = sem("o_full")
        o_free = sem("o_free")
        f_full = sem("f_full")
        f_free = [sem(f"f_free{i}") for i in range(2)]
        xT_ready = sem("xT_ready")
        cT_ready = sem("cT_ready")
        hi_ready = sem("hi_ready")
        rest_ready = sem("rest_ready")
        mid_ready = sem("mid_ready")
        parts_ready = sem("parts_ready")
        stk = [sem(f"stk{i}") for i in range(4)]
        va_ready = sem("va_ready")
        bias_ready = sem("bias_ready")
        sum_ready = sem("sum_ready")
        mx_ready = sem("mx_ready")
        nm_step = sem("nm_step")
        mp_ready = sem("mp_ready")
        sh = [sem(f"sh{i}") for i in range(2)]
        sc_ready = sem("sc_ready")
        pr_ready = sem("pr_ready")
        ot_ready = sem("ot_ready")
        rl_ready = sem("rl_ready")
        X_ready = sem("X_ready")
        XT_ready = sem("XT_ready")
        xb_ready = sem("xb_ready")
        dv = sem("dv")
        ve_ready = sem("ve_ready")
        rstd_ready = sem("rstd_ready")
        x1_ready = sem("x1_ready")
        lg_ready = sem("lg_ready")
        pe_ready = sem("pe_ready")
        gw_ready = sem("gw_ready")
        gwT_ready = sem("gwT_ready")
        ht_ready = sem("ht_ready")
        pv_done = sem("pv_done")
        up_done = sem("up_done")
        dn_done = sem("dn_done")
        y_ready = sem("y_ready")
        nm_ln = sem("nm_ln")
        r_step = sem("r_step")
        stored = sem("stored")

        NFU = 18 + NEXP + 1
        NSU = NT * 5 + NEXP + 1
        NOU = 8
        (F_XT, F_CT, F_Q, F_K, F_V, F_CK, F_CV, F_M, F_X, F_O,
         F_XT1, F_CQ, F_CM, F_CX, F_CO, F_XT2, F_R, F_G, F_DN) = range(19)
        S_BIAS, S_P1, S_P2, S_C1, S_C2, S_UP = 0, NT, 2 * NT, 3 * NT, 4 * NT, 5 * NT
        O_SELF, O_CROSS = 0, 4

        def wait_f(pe, ch, i):
            n = ch * NFU + i
            if n >= 2:
                pe.wait_ge(f_free[n % 2], n // 2)
            return ps_f[n % 2]

        def full_f(e, ch, i):
            n = ch * NFU + i
            e.wait_ge(f_full, n + 1)
            return ps_f[n % 2], f_free[n % 2]

        def wait_s(pe, ch, i):
            n = ch * NSU + i
            if n >= 2:
                pe.wait_ge(s_free[n % 2], n // 2)
            return ps_s[n % 2]

        def full_s(e, ch, i):
            n = ch * NSU + i
            e.wait_ge(s_full, n + 1)
            return ps_s[n % 2], s_free[n % 2]

        def wait_o(pe, ch, i):
            n = ch * NOU + i
            if n >= 1:
                pe.wait_ge(o_free, n)

        def full_o(e, ch, i):
            e.wait_ge(o_full, ch * NOU + i + 1)

        def dve_chain(ch, k):
            return 3 * ch + k + 1

        block = st.enter_context(nc.Block())

        N_WLOADS = 27

        @block.sync
        def _(sp):
            def chunk_loads(ch):
                if ch:
                    sp.wait_ge(xb_ready, 2 * ch - 1)
                    sp.wait_ge(f_full, (ch - 1) * NFU + F_CT + 1)
                sp.dma_start(xin[:, :, :], xv[ch]).then_inc(ld_x, 16)
                sp.dma_start(cin[:, :, :], cv[ch]).then_inc(ld_c, 16)

            chunk_loads(0)
            for i, (w, _) in enumerate(sw + cw):
                sp.dma_start(wnat[:, i, :], w).then_inc(ld_w, 16)
            for i, b in enumerate([sw[0][1], sw[1][1], cw[0][1], cw[1][1]]):
                sp.dma_start(bcol[:, i:i + 1], b.rearrange("(p o) -> p o", o=1)).then_inc(ld_w, 16)
            for i, b in enumerate([sw[2][1], sw[3][1], cw[2][1], cw[3][1]]):
                sp.dma_start(brow[:, i, :], b.rearrange("(o e) -> o e", o=1).broadcast_to([P, E])).then_inc(ld_w, 16)
            sp.dma_start(rb_row[:, :], router_b.rearrange("(o e) -> o e", o=1).broadcast_to([P, NEXP])).then_inc(ld_w, 16)
            sp.dma_start(relx[:, S - 1 - MAX_REL:S + MAX_REL], rel_k.rearrange("r d -> d r"),
                         allow_slow_non_contiguous=True).then_inc(ld_rel, 16)
            sp.dma_start(rel_ext[S - 1 - MAX_REL:S + MAX_REL, :], rel_v).then_inc(ext_done, 16)
            n_end = S - 1 - MAX_REL
            sp.dma_start(rel_ext[0:n_end, :], rel_v[0:1, :].broadcast_to([n_end, HD])).then_inc(ext_done, 16)
            sp.dma_start(rel_ext[S + MAX_REL:WIN, :], rel_v[NREL - 1:NREL, :].broadcast_to([n_end, HD])).then_inc(ext_done, 16)
            sp.wait_ge(ext_done, 48)
            win = bass.AP(rel_ext.tensor, 0, [[HD, P], [HD, S], [1, HD]])
            sp.dma_start(RV[:, :, :], win).then_inc(ld_w, 16)
            for e_, dst in enumerate([hb[:, 0:NEXP, :]]):
                sp.dma_start(dst, rb1.rearrange("e (f p) -> p e f", p=P), allow_slow_non_contiguous=True).then_inc(ld_w, 16)
            sp.dma_start(hb[:, NEXP, :], sb1.rearrange("(f p) -> p f", p=P), allow_slow_non_contiguous=True).then_inc(ld_w, 16)
            sp.dma_start(ob[0:NEXP, :], rb2).then_inc(ld_w, 16)
            sp.dma_start(ob[NEXP:NEXP + 1, :], sb2.rearrange("(o e) -> o e", o=1)).then_inc(ld_w, 16)
            sp.dma_start(w1[:, 0:NEXP, :], rw1.rearrange("e d h -> d e h")).then_inc(ld_w, 16)
            sp.dma_start(w1[:, NEXP, :], sw1).then_inc(ld_w, 16)
            sp.dma_start(w2[:, 0:NEXP, :, :].rearrange("p e f d -> p (e f) d"),
                         rw2.rearrange("e (f p) d -> p (e f) d", p=P)).then_inc(ld_w, 16)
            sp.dma_start(w2[:, NEXP, :, :], sw2.rearrange("(f p) d -> p f d", p=P)).then_inc(ld_w, 16)
            sp.dma_start(wr[:, :], router_w).then_inc(ld_w, 16)
            sp.wait_ge(rel_ready, 3)
            for c in range(NC):
                sp.dma_start(RK[c * HD:(c + 1) * HD, :], relp[:, K_PART[c], :]).then_inc(ld_rk, 16)

            def stack(ch, i, k):
                sp.wait_ge(parts_ready, 2 * (4 * ch + i) + 2)
                dst, parts = (KS if k % 2 else QS)[k // 2], K_PART if k % 2 else Q_PART
                heads = spread[4 * ch + i].rearrange("p (h d) t -> p d h t", d=HD)
                sp.dma_start(spread[4 * ch + i].rearrange("p e t -> e p t"), part[i % 2][:, :, :]).then_inc(spread_out, 16)
                sp.wait_ge(spread_out, 16 * (4 * ch + i + 1))
                for c in range(NC):
                    sp.dma_start(dst[c * HD:(c + 1) * HD, :].rearrange("d (h t) -> d h t", h=H),
                                 heads[parts[c]]).then_inc(stk[k], 16)

            def shifts(ch, a):
                sp.wait_ge(mp_ready, 2 * ch + a + 1)
                for p in range(NSH):
                    for f in range(2):
                        dst = QS[a][KD + p:KD + p + 1, f * 4096:(f + 1) * 4096]
                        sp.dma_start(dst.rearrange("o (r i) -> o r i", i=32), MP[:, p, f, :]).then_inc(sh[a], 16)

            for ch in range(NCH):
                if ch:
                    sp.wait_ge(s_full, (ch - 1) * NSU + S_P2 + NT)
                stack(ch, 0, 0)
                stack(ch, 1, 1)
                if ch:
                    sp.wait_ge(s_full, (ch - 1) * NSU + S_C2 + NT)
                stack(ch, 2, 3)
                shifts(ch, 0)
                stack(ch, 3, 2)
                if ch + 1 < NCH:
                    chunk_loads(ch + 1)
                shifts(ch, 1)
                sp.wait_ge(y_ready, ch + 1)
                sp.dma_start(ov[ch], x1[:, :, :]).then_inc(stored, 16)
            sp.wait_ge(stored, 16 * NCH)

        @block.gpsimd
        def _(g):
            nc.gpsimd.memset(ident[:, :], 0.0).then_inc(c_pool, 1)
            nc.gpsimd.memset(maskT[:, :, :], 0.0).then_inc(c_pool, 1)
            nc.gpsimd.memset(tri[:, :, :], 1.0).then_inc(c_pool, 1)
            g.wait_ge(c_pool, 3)
            nc.gpsimd.affine_select(out=ident[:, :], in_=ident[:, :], compare_op=ALU.not_equal, fill=1.0,
                                    base=0, pattern=[[-1, P]], channel_multiplier=1).then_inc(c_pool, 1)
            nc.gpsimd.affine_select(out=maskT[:, :, :], in_=maskT[:, :, :], compare_op=ALU.is_ge, fill=MASKED,
                                    base=0, pattern=[[0, 4], [1, S]], channel_multiplier=-1).then_inc(c_pool, 1)
            nc.gpsimd.affine_select(out=tri[:, :, :], in_=tri[:, :, :], compare_op=ALU.is_gt, fill=0.0,
                                    base=0, pattern=[[1, NEXP], [-1, NEXP]], channel_multiplier=0).then_inc(c_pool, 1)
            g.wait_ge(c_pool, 6)
            nc.gpsimd.tensor_copy(identb[:, :], ident[:, :]).then_inc(c_pool, 1)
            nc.gpsimd.memset(epst[:, :], EPS).then_inc(c_pool, 1)
            nc.gpsimd.memset(halfm[:, :], -0.5).then_inc(c_pool, 1)

            def split_rest(ch, i):
                n = 4 * ch + i
                g.wait_ge(rest_ready, n + 1)
                nc.gpsimd.tensor_copy(part[i % 2][:, 1, :], rest[i % 2][:, :]).then_inc(parts_ready, 1)
                g.wait_ge(parts_ready, 2 * n + 1)
                nc.gpsimd.tensor_tensor(part[i % 2][:, 2, :], rest[i % 2][:, :], part[i % 2][:, 1, :],
                                        ALU.subtract).then_inc(parts_ready, 1)

            def residual(ch, a):
                src = xin if a == 0 else x1
                if a == 0:
                    g.wait_ge(ld_x, 16 * (ch + 1))
                    if ch:
                        g.wait_ge(dv, dve_chain(ch - 1, 1))
                else:
                    g.wait_ge(x1_ready, 2 * ch + 1)
                nc.gpsimd.tensor_tensor(xb[:, :, :], src[:, :, :],
                                        brow[:, 2 * a + 1:2 * a + 2, :].broadcast_to([P, NB, E]),
                                        ALU.add).then_inc(xb_ready, 1)

            def root(ch, a):
                g.wait_ge(ve_ready, 3 * ch + a + 1)
                nc.gpsimd.tensor_tensor(ve[:, :], mv[:, :, 1], epst[:, :], ALU.add).then_inc(rstd_ready, 1)
                g.wait_ge(rstd_ready, 2 * (3 * ch + a) + 1)
                nc.gpsimd.tensor_tensor(rstd[:, :], ve[:, :], halfm[:, :], ALU.pow).then_inc(rstd_ready, 1)

            g.wait_ge(ld_w, 16 * N_WLOADS)
            for ch in range(NCH):
                residual(ch, 0)
                for i in range(3):
                    split_rest(ch, i)
                root(ch, 0)
                residual(ch, 1)
                split_rest(ch, 3)
                root(ch, 1)
                root(ch, 2)

        @block.tensor
        def _(pe):
            pe.wait_ge(c_pool, 9)
            pe.wait_ge(ld_w, 16 * N_WLOADS)
            for i in range(8):
                nc.tensor.transpose(ps_s[i // 4][:, (i % 4) * P:(i % 4 + 1) * P], wnat[:, i, :],
                                    ident[:, :]).then_inc(wt_ps, 1)
            pe.wait_ge(wt_sb, 2)
            pe.wait_ge(c_dve, 4)

            def transposes(ch, i, src):
                ps = wait_f(pe, ch, i)
                for b in range(NB):
                    last = nc.tensor.transpose(ps[:, b * S:(b + 1) * S], src(b), ident[:, :])
                last.then_inc(f_full, 1)

            def project(ch, i, w, src):
                ps = wait_f(pe, ch, i)
                nc.tensor.matmul(ps[:, :], wT[:, w, :], src[:, :], start=True, stop=True).then_inc(f_full, 1)

            def rows(ch, i, w, src):
                ps = wait_f(pe, ch, i)
                for b in range(NB):
                    last = nc.tensor.matmul(ps[:, b * E:(b + 1) * E], src[:, b * S:(b + 1) * S], wT[:, w, :],
                                            start=True, stop=True)
                last.then_inc(f_full, 1)

            def scores(ch, base, a, kd, masked):
                for t in range(NT):
                    ps = wait_s(pe, ch, base + t)
                    for half in range(2):
                        if masked:
                            nc.tensor.matmul(ps[:, half * BANK:(half + 1) * BANK], identb[:, :],
                                             maskT[:, :, :].rearrange("p a q -> p (a q)"), start=True, stop=False,
                                             skip_group_check=True)
                        for j in range(4):
                            c = (t * HB_TILE + half * 4 + j) * S
                            o = (half * 4 + j) * S
                            last = nc.tensor.matmul(ps[:, o:o + S], KS[a][0:kd, c:c + S], QS[a][0:kd, c:c + S],
                                                    start=not masked and j == 0, stop=j == 3, skip_group_check=True)
                    last.then_inc(s_full, 1)

            def maxima(ch, i, n):
                pe.wait_ge(mx_ready, n * NT + NT)
                ps = wait_f(pe, ch, i)
                for f in range(2):
                    last = nc.tensor.transpose(ps[:, f * P:(f + 1) * P], MX[:, f * P:(f + 1) * P], ident[:, :])
                last.then_inc(f_full, 1)

            def heads_to_tokens(ch, base, view):
                for i in range(2):
                    wait_o(pe, ch, base + 2 + i)
                    for j in range(8):
                        last = nc.tensor.transpose(ps_o[:, j * P:(j + 1) * P], view(8 * i + j), ident[:, :])
                    last.then_inc(o_full, 1)

            def attention_out(ch, a):
                pe.wait_ge(X_ready, 2 * (2 * ch + a) + 2)
                transposes(ch, F_CX if a else F_X, lambda b: X[:, b, :, :].rearrange("p h d -> p (h d)"))
                pe.wait_ge(XT_ready, 2 * ch + a + 1)
                rows(ch, F_CO if a else F_O, 4 * a + 3, XT)

            for ch in range(NCH):
                pe.wait_ge(ld_x, 16 * (ch + 1))
                transposes(ch, F_XT, lambda b: xin[:, b, :])
                pe.wait_ge(ld_c, 16 * (ch + 1))
                transposes(ch, F_CT, lambda b: cin[:, b, :])
                pe.wait_ge(xT_ready, 3 * ch + 1)
                project(ch, F_Q, 0, actT)
                project(ch, F_K, 1, actT)
                rows(ch, F_V, 2, actT)
                pe.wait_ge(cT_ready, ch + 1)
                project(ch, F_CK, 5, ctxT)
                rows(ch, F_CV, 6, ctxT)
                pe.wait_ge(stk[0], 16 * NC * (ch + 1))
                pe.wait_ge(ld_rk, 16 * NC)
                qv = QS[0][0:KD, :].rearrange("k (g q) -> k g q", q=S)
                for t in range(NT):
                    ps = wait_s(pe, ch, S_BIAS + t)
                    for j in range(S // NT):
                        q = t * (S // NT) + j
                        last = nc.tensor.matmul(ps[:, j * HB:(j + 1) * HB], RK[:, S - 1 - q:2 * S - 1 - q],
                                                qv[:, :, q], start=True, stop=True)
                    last.then_inc(s_full, 1)
                pe.wait_ge(stk[1], 16 * NC * (ch + 1))
                scores(ch, S_P1, 0, KD, False)
                maxima(ch, F_M, 2 * ch)
                pe.wait_ge(sh[0], 16 * 6 * (ch + 1))
                scores(ch, S_P2, 0, KD2, False)
                pe.wait_ge(va_ready, 2 * ch + 1)
                pe.wait_ge(pr_ready, 2 * ch * NT + NT)
                pv = ST[:, :].rearrange("p (h b q) -> p h b q", h=H, b=NB)
                for half in range(2):
                    wait_o(pe, ch, O_SELF + half)
                    o = ps_o[:, :].rearrange("p (q h) -> p q h", h=H)
                    for q4 in range(2):
                        q0, r0 = half * 64 + q4 * 32, q4 * 32
                        for h in range(H):
                            for b in range(NB):
                                nc.tensor.matmul(o[b * PAD:(b + 1) * PAD, r0:r0 + 32, h], VA[0][:, b, h, :],
                                                 pv[:, h, b, q0:q0 + 32], start=h == 0, stop=False,
                                                 tile_position=(0, b * PAD), skip_group_check=True)
                        for j in range(32):
                            for b in range(NB):
                                last = nc.tensor.matmul(o[b * PAD:b * PAD + HD, r0 + j, :],
                                                        RV[:, S - 1 - (q0 + j), :], pv[:, :, b, q0 + j],
                                                        start=False, stop=j == 31, tile_position=(0, b * PAD),
                                                        skip_group_check=True)
                    last.then_inc(o_full, 1)
                pe.wait_ge(ot_ready, 2 * (2 * ch) + 2)
                otv = OT[:, :].rearrange("p (q h) -> p q h", h=H)
                heads_to_tokens(ch, O_SELF, lambda h: otv[:, :, h])
                attention_out(ch, 0)
                pe.wait_ge(x1_ready, 2 * ch + 1)
                transposes(ch, F_XT1, lambda b: x1[:, b, :])
                pe.wait_ge(xT_ready, 3 * ch + 2)
                project(ch, F_CQ, 4, actT)
                pe.wait_ge(stk[2], 16 * NC * (ch + 1))
                pe.wait_ge(stk[3], 16 * NC * (ch + 1))
                scores(ch, S_C1, 1, KD, True)
                maxima(ch, F_CM, 2 * ch + 1)
                pe.wait_ge(sh[1], 16 * 6 * (ch + 1))
                scores(ch, S_C2, 1, KD2, True)
                pe.wait_ge(va_ready, 2 * ch + 2)
                pe.wait_ge(pr_ready, 2 * ch * NT + 2 * NT)
                for half in range(2):
                    wait_o(pe, ch, O_CROSS + half)
                    for h in range(8 * half, 8 * half + 8):
                        for b in range(NB):
                            last = nc.tensor.matmul(ps_o[b * PAD:(b + 1) * PAD, (h % 8) * S:(h % 8 + 1) * S],
                                                    VA[1][:, b, h, :], pv[:, h, b, :], start=h % 4 == 0,
                                                    stop=h % 4 == 3, tile_position=(0, b * PAD),
                                                    skip_group_check=True)
                    last.then_inc(o_full, 1)
                pe.wait_ge(ot_ready, 2 * (2 * ch + 1) + 2)
                heads_to_tokens(ch, O_CROSS, lambda h: OT[:, h * S:(h + 1) * S])
                attention_out(ch, 1)
                pe.wait_ge(x1_ready, 2 * ch + 2)
                transposes(ch, F_XT2, lambda b: x1[:, b, :])
                pe.wait_ge(xT_ready, 3 * ch + 3)
                ps = wait_f(pe, ch, F_R)
                for b in range(NB):
                    last = nc.tensor.matmul(ps[:, b * NEXP:(b + 1) * NEXP], actT[:, b * S:(b + 1) * S], wr[:, :],
                                            start=True, stop=True)
                last.then_inc(f_full, 1)

                def up(i, e):
                    ps = wait_s(pe, ch, S_UP + i)
                    for f in range(NF):
                        last = nc.tensor.matmul(ps[:, f * T:(f + 1) * T], w1[:, e, f * P:(f + 1) * P], actT[:, :],
                                                start=True, stop=True)
                    last.then_inc(s_full, 1)

                def down(i, e):
                    n = ch * (NEXP + 1) + i
                    pe.wait_ge(ht_ready, n + 1)
                    ps = wait_f(pe, ch, F_DN + i)
                    for b in range(NB):
                        for f in range(NF):
                            last = nc.tensor.matmul(ps[:, b * E:(b + 1) * E], HT[n % 2][:, f, b * S:(b + 1) * S],
                                                    w2[:, e, f, :], start=f == 0, stop=f == NF - 1 and i > 0)
                        if i == 0:
                            last = nc.tensor.matmul(ps[:, b * E:(b + 1) * E], gwT[:, b, :], ob[:, :],
                                                    start=False, stop=True)
                    last.then_inc(f_full, 1)

                up(0, NEXP)
                up(1, 0)
                pe.wait_ge(gw_ready, ch + 1)
                ps = wait_f(pe, ch, F_G)
                for b in range(NB):
                    last = nc.tensor.transpose(ps[0:PAD, b * S:(b + 1) * S], gw[:, b, :], ident[:, :])
                last.then_inc(f_full, 1)
                pe.wait_ge(gwT_ready, ch + 1)
                down(0, NEXP)
                for i in range(1, NEXP + 1):
                    if i < NEXP:
                        up(i + 1, i)
                    down(i, i - 1)

        @block.scalar
        def _(act):
            for i in range(2):
                act.wait_ge(wt_ps, 4 * (i + 1))
                nc.scalar.copy(wT[:, 4 * i:4 * i + 4, :].rearrange("p w o -> p (w o)"), ps_s[i][:, 0:BANK]).then_inc(wt_sb, 1)

            def high(ch, f, i, b):
                ps, _ = full_f(act, ch, f)
                n = 4 * ch + i
                if n >= 2:
                    act.wait_ge(stk[[0, 1, 3, 2][(i - 2) % 4]], 16 * NC * (ch + 1 if i >= 2 else ch))
                nc.scalar.activation(part[i % 2][:, 0, :], ps[:, :], ACT.Identity, bias=bcol[:, b:b + 1]).then_inc(hi_ready, 1)

            def out_heads(ch, base, i0):
                for i in range(2):
                    full_o(act, ch, base + i)
                    nc.scalar.copy(OT[:, i * TILE:(i + 1) * TILE], ps_o[:, :]).then_inc(ot_ready, 1)
                    act.wait_ge(ot_ready, 2 * (2 * ch + i0) + i + 1)
                    act.sem_inc(o_free, 1)

            for ch in range(NCH):
                def copy_f(dst, f, s):
                    ps, free = full_f(act, ch, f)
                    nc.scalar.copy(dst, ps[:, :]).then_inc(s, 1)
                    return free

                def released(s, v, free):
                    act.wait_ge(s, v)
                    act.sem_inc(free, 1)

                released(xT_ready, 3 * ch + 1, copy_f(actT[:, :], F_XT, xT_ready))
                released(cT_ready, ch + 1, copy_f(ctxT[:, :], F_CT, cT_ready))
                high(ch, F_Q, 0, 0)
                high(ch, F_K, 1, 1)
                high(ch, F_CK, 2, 3)
                for t in range(NT):
                    ps, free = full_s(act, ch, S_BIAS + t)
                    nq = S // NT
                    dst = ST[:, :].rearrange("p (g q) -> p g q", q=S)[:, :, t * nq:(t + 1) * nq]
                    nc.scalar.copy(dst, ps[:, :].rearrange("p (q g) -> p g q", g=HB)).then_inc(bias_ready, 1)
                    act.wait_ge(bias_ready, ch * NT + t + 1)
                    act.sem_inc(free, 1)
                for t in range(NT):
                    act.wait_ge(sc_ready, ch * NT + t + 1)
                    v = ST[:, t * TILE:(t + 1) * TILE]
                    nc.scalar.activation(v, v, ACT.Exp, scale=SCALE).then_inc(pr_ready, 1)
                out_heads(ch, O_SELF, 0)
                released(XT_ready, 2 * ch + 1, copy_f(XT[:, :], F_X, XT_ready))
                released(xT_ready, 3 * ch + 2, copy_f(actT[:, :], F_XT1, xT_ready))
                high(ch, F_CQ, 3, 2)
                for t in range(NT):
                    ps, free = full_s(act, ch, S_C2 + t)
                    nc.scalar.activation(ST[:, t * TILE:(t + 1) * TILE], ps[:, :], ACT.Exp, scale=SCALE).then_inc(pr_ready, 1)
                    act.wait_ge(pr_ready, 2 * ch * NT + NT + t + 1)
                    act.sem_inc(free, 1)
                out_heads(ch, O_CROSS, 1)
                released(XT_ready, 2 * ch + 2, copy_f(XT[:, :], F_CX, XT_ready))
                released(xT_ready, 3 * ch + 3, copy_f(actT[:, :], F_XT2, xT_ready))
                act.wait_ge(lg_ready, ch + 1)
                nc.scalar.activation(pe_[:, :, :], lg[:, :, :], ACT.Exp).then_inc(pe_ready, 1)
                for i in range(NEXP + 1):
                    e = NEXP if i == 0 else i - 1
                    ps, free = full_s(act, ch, S_UP + i)
                    n = ch * (NEXP + 1) + i
                    if n >= 2:
                        act.wait_ge(dn_done, n - 1)
                    for f in range(NF):
                        last = nc.scalar.activation(HT[n % 2][:, f, :], ps[:, f * T:(f + 1) * T], ACT.Gelu,
                                                    bias=hb[:, e, f:f + 1])
                    last.then_inc(ht_ready, 1)
                    act.wait_ge(ht_ready, n + 1)
                    act.sem_inc(free, 1)

        @block.vector
        def _(v):
            for a in range(2):
                nc.vector.memset(KS[a][32:KD2, :], 1.0)
                nc.vector.memset(VA[a][:, :, :, :], 0.0).then_inc(c_dve, 1)
            v.wait_ge(c_dve, 2)
            for a in range(2):
                nc.vector.memset(VA[a][:, :, :, HD:HD + 1], 1.0).then_inc(c_dve, 1)
            nc.vector.memset(gw[:, :, :], 0.0).then_inc(c_dve, 1)
            v.wait_ge(c_dve, 5)
            nc.vector.memset(gw[:, :, NEXP:NEXP + 1], 1.0).then_inc(c_dve, 1)
            v.wait_ge(ld_rel, 16)
            n_end = S - 1 - MAX_REL
            nc.vector.tensor_copy(relx[:, 0:n_end], relx[:, n_end:n_end + 1].broadcast_to([HD, n_end]))
            nc.vector.tensor_copy(relx[:, S + MAX_REL:WPAD],
                                  relx[:, S + MAX_REL - 1:S + MAX_REL].broadcast_to([HD, WPAD - S - MAX_REL])).then_inc(c_dve, 1)
            v.wait_ge(c_dve, 7)
            nc.vector.tensor_copy(relp[:, 0, :], relx[:, :]).then_inc(rel_ready, 1)
            v.wait_ge(rel_ready, 1)
            nc.vector.tensor_tensor(relr[:, :], relx[:, :], relp[:, 0, :], ALU.subtract).then_inc(c_dve, 1)
            v.wait_ge(c_dve, 8)
            nc.vector.tensor_copy(relp[:, 1, :], relr[:, :]).then_inc(rel_ready, 1)
            v.wait_ge(rel_ready, 2)
            nc.vector.tensor_tensor(relp[:, 2, :], relr[:, :], relp[:, 1, :], ALU.subtract).then_inc(rel_ready, 1)
            v.wait_ge(ld_w, 16 * N_WLOADS)

            def left(ch, f, i, b):
                ps, free = full_f(v, ch, f)
                v.wait_ge(hi_ready, 4 * ch + i + 1)
                if 4 * ch + i >= 2:
                    v.wait_ge(parts_ready, 2 * (4 * ch + i - 1))
                nc.vector.scalar_tensor_tensor(rest[i % 2][:, :], ps[:, :], bcol[:, b:b + 1], part[i % 2][:, 0, :],
                                               ALU.add, ALU.subtract).then_inc(rest_ready, 1)
                v.wait_ge(rest_ready, 4 * ch + i + 1)
                v.sem_inc(free, 1)

            def values(ch, f, a):
                ps, free = full_f(v, ch, f)
                nc.vector.tensor_tensor(VA[a][:, :, :, 0:HD],
                                        ps[:, :].rearrange("p (b h d) -> p b h d", b=NB, h=H),
                                        brow[:, 2 * a:2 * a + 1, :].rearrange("p o (h d) -> p o h d", h=H)
                                        .broadcast_to([P, NB, H, HD]), ALU.add).then_inc(va_ready, 1)
                v.wait_ge(va_ready, 2 * ch + a + 1)
                v.sem_inc(free, 1)

            def tile_max(n, t, src):
                nc.vector.tensor_reduce(MX[:, t * 32:(t + 1) * 32], src.rearrange("p (c i) -> p c i", i=32),
                                        AXIS.X, ALU.max, apply_transpose=True).then_inc(mx_ready, 1)

            def shift_parts(ch, f, a):
                ps, free = full_f(v, ch, f)
                n = 2 * ch + a
                nc.vector.tensor_reduce(NM[:, :, :], ps[:, 0:256].rearrange("p (f a i) -> p f i a", f=2, a=4),
                                        AXIS.X, ALU.max, negate=True).then_inc(nm_step, 1)
                v.wait_ge(nm_step, 4 * n + 1)
                v.sem_inc(free, 1)
                if n:
                    v.wait_ge(sh[1 - a], 16 * 6 * (ch if a == 0 else ch + 1))
                nc.vector.tensor_copy(MP[:, 0, :, :], NM[:, :, :]).then_inc(nm_step, 1)
                v.wait_ge(nm_step, 4 * n + 2)
                nc.vector.tensor_tensor(NR[:, :, :], NM[:, :, :], MP[:, 0, :, :], ALU.subtract).then_inc(nm_step, 1)
                v.wait_ge(nm_step, 4 * n + 3)
                nc.vector.tensor_copy(MP[:, 1, :, :], NR[:, :, :]).then_inc(nm_step, 1)
                v.wait_ge(nm_step, 4 * n + 4)
                nc.vector.tensor_tensor(MP[:, 2, :, :], NR[:, :, :], MP[:, 1, :, :], ALU.subtract).then_inc(mp_ready, 1)

            def normalise(ch, base, a):
                for i in range(2):
                    full_o(v, ch, base + 2 + i)
                    n = 2 * (2 * ch + a) + i
                    o = ps_o[:, :].rearrange("p (h b d) -> p h b d", h=8, b=NB)
                    nc.vector.reciprocal(rl[:, i, :, :], o[:, :, :, HD]).then_inc(rl_ready, 1)
                    v.wait_ge(rl_ready, n + 1)
                    nc.vector.tensor_tensor(X[:, :, 8 * i:8 * i + 8, :].rearrange("p b h d -> p h b d"),
                                            o[:, :, :, 0:HD],
                                            rl[:, i, :, :].rearrange("p h (b o) -> p h b o", o=1)
                                            .broadcast_to([P, 8, NB, HD]), ALU.mult).then_inc(X_ready, 1)
                    v.wait_ge(X_ready, n + 1)
                    v.sem_inc(o_free, 1)

            def layer_norm(ch, k, y, done):
                v.wait_ge(dv, 3 * ch + k + 1)
                for b in range(NB):
                    last = nc.vector.bn_stats(stats[:, b, :], y[:, b, :])
                last.then_inc(nm_ln, 1)
                v.wait_ge(nm_ln, 3 * ch + k + 1)
                for b in range(NB):
                    last = nc.vector.bn_aggr(mv[:, b, :], stats[:, b, :])
                last.then_inc(ve_ready, 1)
                v.wait_ge(rstd_ready, 2 * (3 * ch + k) + 2)
                for b in range(NB):
                    last = nc.vector.tensor_scalar(x1[:, b, :], y[:, b, :], mv[:, b, 0:1], rstd[:, b:b + 1],
                                                   ALU.subtract, ALU.mult)
                last.then_inc(done, 1)

            for ch in range(NCH):
                left(ch, F_Q, 0, 0)
                left(ch, F_K, 1, 1)
                values(ch, F_V, 0)
                left(ch, F_CK, 2, 3)
                values(ch, F_CV, 1)
                v.wait_ge(bias_ready, NT * (ch + 1))
                for t in range(NT):
                    ps, free = full_s(v, ch, S_P1 + t)
                    nc.vector.tensor_tensor(SUM[:, t % 2, :], ps[:, :], ST[:, t * TILE:(t + 1) * TILE],
                                            ALU.add).then_inc(sum_ready, 1)
                    v.wait_ge(sum_ready, ch * NT + t + 1)
                    v.sem_inc(free, 1)
                    tile_max(2 * ch, t, SUM[:, t % 2, :])
                shift_parts(ch, F_M, 0)
                for t in range(NT):
                    ps, free = full_s(v, ch, S_P2 + t)
                    w = ST[:, t * TILE:(t + 1) * TILE]
                    nc.vector.tensor_tensor(w, ps[:, :], w, ALU.add).then_inc(sc_ready, 1)
                    v.wait_ge(sc_ready, ch * NT + t + 1)
                    v.sem_inc(free, 1)
                normalise(ch, O_SELF, 0)
                ps, free = full_f(v, ch, F_O)
                v.wait_ge(xb_ready, 2 * ch + 1)
                nc.vector.tensor_tensor(Y[:, :, :].rearrange("p b e -> p (b e)"), ps[:, :],
                                        xb[:, :, :].rearrange("p b e -> p (b e)"), ALU.add).then_inc(dv, 1)
                v.wait_ge(dv, 3 * ch + 1)
                v.sem_inc(free, 1)
                if ch:
                    v.wait_ge(stored, 16 * ch)
                layer_norm(ch, 0, Y, x1_ready)
                left(ch, F_CQ, 3, 2)
                for t in range(NT):
                    ps, free = full_s(v, ch, S_C1 + t)
                    tile_max(2 * ch + 1, t, ps[:, :])
                    v.wait_ge(mx_ready, (2 * ch + 1) * NT + t + 1)
                    v.sem_inc(free, 1)
                shift_parts(ch, F_CM, 1)
                normalise(ch, O_CROSS, 1)
                ps, free = full_f(v, ch, F_CO)
                v.wait_ge(xb_ready, 2 * ch + 2)
                nc.vector.tensor_tensor(Y[:, :, :].rearrange("p b e -> p (b e)"), ps[:, :],
                                        xb[:, :, :].rearrange("p b e -> p (b e)"), ALU.add).then_inc(dv, 1)
                v.wait_ge(dv, 3 * ch + 2)
                v.sem_inc(free, 1)
                layer_norm(ch, 1, Y, x1_ready)
                ps, free = full_f(v, ch, F_R)
                nc.vector.tensor_tensor(lg[:, :, :], ps[:, 0:NB * NEXP].rearrange("p (b e) -> p b e", b=NB),
                                        rb_row[:, :].rearrange("p (o e) -> p o e", o=1).broadcast_to([P, NB, NEXP]),
                                        ALU.add).then_inc(r_step, 1)
                r = 9 * ch
                v.wait_ge(r_step, r + 1)
                v.sem_inc(free, 1)
                nc.vector.tensor_reduce(lmax[:, :], lg[:, :, :], AXIS.X, ALU.max).then_inc(r_step, 1)
                v.wait_ge(r_step, r + 2)

                def over(a):
                    return a[:, :].rearrange("p (b o) -> p b o", o=1).broadcast_to([P, NB, NEXP])
                nc.vector.tensor_tensor(lg[:, :, :], lg[:, :, :], over(lmax), ALU.subtract).then_inc(lg_ready, 1)
                v.wait_ge(pe_ready, ch + 1)
                nc.vector.tensor_reduce(lsum[:, :], pe_[:, :, :], AXIS.X, ALU.add).then_inc(r_step, 1)
                v.wait_ge(r_step, r + 3)
                nc.vector.reciprocal(lmax[:, :], lsum[:, :]).then_inc(r_step, 1)
                v.wait_ge(r_step, r + 4)
                nc.vector.tensor_tensor(pe_[:, :, :], pe_[:, :, :], over(lmax), ALU.mult).then_inc(r_step, 1)
                v.wait_ge(r_step, r + 5)
                pj = pe_[:, :, :].rearrange("p b (o j) -> p b o j", o=1).broadcast_to([P, NB, NEXP, NEXP])
                pi = pe_[:, :, :].rearrange("p b (e o) -> p b e o", o=1).broadcast_to([P, NB, NEXP, NEXP])
                nc.vector.tensor_tensor(gt[:, :, :, :], pj, pi, ALU.is_gt)
                nc.vector.tensor_tensor(eq[:, :, :, :], pj, pi, ALU.is_equal).then_inc(r_step, 1)
                v.wait_ge(r_step, r + 6)
                tb = tri[:, :, :].rearrange("p (o e) j -> p o e j", o=1).broadcast_to([P, NB, NEXP, NEXP])
                nc.vector.tensor_tensor(eq[:, :, :, :], eq[:, :, :, :], tb, ALU.mult).then_inc(r_step, 1)
                v.wait_ge(r_step, r + 7)
                nc.vector.tensor_tensor(gt[:, :, :, :], gt[:, :, :, :], eq[:, :, :, :], ALU.add).then_inc(r_step, 1)
                v.wait_ge(r_step, r + 8)
                nc.vector.tensor_reduce(rank[:, :, :], gt[:, :, :, :], AXIS.X, ALU.add).then_inc(r_step, 1)
                v.wait_ge(r_step, r + 9)
                nc.vector.scalar_tensor_tensor(gw[:, :, 0:NEXP], rank[:, :, :], float(TOP_K), pe_[:, :, :],
                                               ALU.is_lt, ALU.mult).then_inc(gw_ready, 1)
                ps, free = full_f(v, ch, F_G)
                nc.vector.tensor_copy(gwT[:, :, :].rearrange("p b t -> p (b t)"), ps[0:NEXP + 1, :]).then_inc(gwT_ready, 1)
                v.wait_ge(gwT_ready, ch + 1)
                v.sem_inc(free, 1)
                for i in range(NEXP + 1):
                    n = ch * (NEXP + 1) + i
                    ps, free = full_f(v, ch, F_DN + i)
                    if i:
                        v.wait_ge(dn_done, n)
                    if i == 0:
                        nc.vector.tensor_tensor(acc[:, :, :].rearrange("p b e -> p (b e)"), ps[:, :],
                                                x1[:, :, :].rearrange("p b e -> p (b e)"), ALU.add).then_inc(dn_done, 1)
                    else:
                        for b in range(NB):
                            last = nc.vector.scalar_tensor_tensor(acc[:, b, :], ps[:, b * E:(b + 1) * E],
                                                                  gw[:, b, i - 1:i], acc[:, b, :],
                                                                  ALU.mult, ALU.add)
                        last.then_inc(dn_done, 1)
                    v.wait_ge(dn_done, n + 1)
                    v.sem_inc(free, 1)
                nc.vector.engine_nop().then_inc(dv, 1)
                layer_norm(ch, 2, acc, y_ready)


_ATTN = ["Wq", "bq", "Wk", "bk", "Wv", "bv", "Wo", "bo"]
_INS = (["x", "ctx_1024"] + [f"L0_attn_{n}" for n in _ATTN] + ["L0_attn_rel_k", "L0_attn_rel_v"]
        + [f"L0_xattn_{n}" for n in _ATTN]
        + [f"L0_ffn_{n}" for n in ["router_w", "router_b", "sw1", "sb1", "sw2", "sb2", "rw1", "rb1", "rw2", "rb2"]])


def kernel(**inputs):
    import numpy as np
    import concourse.bacc as bacc
    from concourse.bass_utils import run_bass_kernel_spmd as run

    nc = bacc.Bacc("TRN2", target_bir_lowering=False, num_devices=1)
    arrays, ap = {}, {}
    for name in _INS:
        a = np.ascontiguousarray(inputs[name])
        arrays[f"in_{name}"] = a
        ap[name] = nc.dram_tensor(f"in_{name}", a.shape, mybir.dt.from_np(a.dtype), kind="ExternalInput").ap()
    out = nc.dram_tensor("out_x", inputs["x"].shape, mybir.dt.float32, kind="ExternalOutput").ap()
    rel_ext = nc.dram_tensor("rel_v_by_distance", (WIN, HD), mybir.dt.float32, kind="Internal").ap()

    spread = nc.dram_tensor("parts_by_head", (4 * (inputs['x'].shape[0] // NB), 3, E, T), mybir.dt.bfloat16, kind="Internal").ap()

    def layer(p):
        return [(ap[f"{p}_W{n}"], ap[f"{p}_b{n}"]) for n in "qkvo"]
    f = {n[7:]: a for n, a in ap.items() if n.startswith("L0_ffn_")}
    build(nc, ap["x"], ap["ctx_1024"], layer("L0_attn"), layer("L0_xattn"), ap["L0_attn_rel_k"],
          ap["L0_attn_rel_v"], f["router_w"], f["router_b"], f["sw1"], f["sb1"], f["sw2"], f["sb2"],
          f["rw1"], f["rb1"], f["rw2"], f["rb2"], rel_ext, spread, out)
    r = run(nc, [arrays], core_ids=[0])
    return r.results[0]["out_x"]
```

```python
import concourse.bass as bass
from concourse import mybir
from contextlib import ExitStack

F32 = mybir.dt.float32
BF16 = mybir.dt.bfloat16
U32 = mybir.dt.uint32
ACT = mybir.ActivationFunctionType
ALU = mybir.AluOpType
AXIS = mybir.AxisListType

P = 128
S = 128
E = 128
H = 16
HD = E // H
MAX_REL = 20
NREL = 2 * MAX_REL + 1
NB = 4
T = NB * S
HB = H * NB
HB_TILE = 8
TILE = HB_TILE * S
NT = HB // HB_TILE
BANK = 512
NQ = 4
QD = P // NQ
HQ = H // NQ
NEXP = 8
TOP_K = 2
HID = 256
NF = HID // P
NPC = 3
WIN = 2 * S - 1
WPAD = 256
EPS = 1e-5
TWO_ONES = 1.0019378662109375
SCALE = float(HD) ** -0.5
MASKED = -1.0e30

Q_PART = [0, 1, 2, 0, 1, 0]
K_PART = [0, 1, 0, 1, 0, 2]
NC = len(Q_PART)
KD = NC * HD
KZ = 65
NSH = 3
KD2 = KZ + NSH


def runs(parts):
    out = []
    for c, p in enumerate(parts):
        if out and out[-1][1] + out[-1][2] == p and out[-1][0] + out[-1][2] == c:
            out[-1][2] += 1
        else:
            out.append([c, p, 1])
    return out


CHUNK_AT = [0.00, 96.90, 193.76, 290.58]
PLACE = {
    "xT": (1, 0.00, 0.000),
    "q": (1, 3.72, 0.000),
    "k": (1, 10.00, 0.000),
    "v": (1, 22.29, 0.000),
    "bias": (NT, 30.91, 0.322),
    "p1": (NT, 37.32, 3.822),
    "cT": (1, 62.70, 0.000),
    "m": (1, 67.38, 0.000),
    "p2": (NT, 72.17, 1.484),
    "pv": (NQ, 78.53, 3.833),
    "cv": (1, 84.20, 0.000),
    "pvT": (NQ, 87.34, 2.757),
    "ck": (1, 87.45, 0.000),
    "w2": (NQ, 92.18, 1.251),
    "w2T": (NQ, 100.43, 0.050),
    "X": (1, 106.09, 0.000),
    "XT": (1, 109.16, 0.000),
    "o": (1, 113.46, 0.000),
    "ln": (1, 114.54, 0.000),
    "x1T": (1, 123.23, 0.000),
    "cq": (1, 123.94, 0.000),
    "c1": (NT, 140.59, 0.050),
    "cm": (1, 142.77, 0.000),
    "c2": (NT, 155.26, 1.817),
    "cpv": (NQ, 161.12, 3.657),
    "cpvT": (NQ, 167.68, 3.349),
    "cX": (1, 181.19, 0.000),
    "cXT": (1, 184.47, 0.000),
    "co": (1, 187.75, 0.000),
    "cln": (1, 189.56, 0.000),
    "x2T": (1, 192.41, 0.000),
    "r": (1, 192.58, 0.000),
    "up": (NEXP + 1, 195.47, 6.328),
    "g": (1, 202.61, 0.000),
    "dn": (NEXP + 1, 204.73, 6.824),
    "fln": (1, 300.37, 0.000),
}
F_STEPS = {"xT", "q", "k", "v", "m", "pv", "w2", "pvT", "w2T", "XT", "o", "cT", "ck", "cv", "x1T", "cq", "cm",
           "cpv", "cpvT", "cXT", "co", "x2T", "r", "g", "dn"}
S_STEPS = {"bias", "p1", "p2", "c1", "c2", "up"}


def build(nc, x, ctx, sw, cw, rel_k, rel_v, router_w, router_b, sw1, sb1, sw2, sb2,
          rw1, rb1, rw2, rb2, rel_ext, spread, out):
    NCH = x.shape[0] // NB
    xv = x.rearrange("(c b) s e -> c s b e", b=NB)
    cv = ctx.rearrange("(c b) s e -> c s b e", b=NB)
    ov = out.rearrange("(c b) s e -> c s b e", b=NB)

    ORDER = []
    for c in range(NCH):
        for w, (n, first, apart) in PLACE.items():
            ORDER += [(CHUNK_AT[c] + first + apart * t, c, w, t) for t in range(n)]
    ORDER = [s[1:] for s in sorted(ORDER)]
    F_USES = [s for s in ORDER if s[1] in F_STEPS]
    S_USES = [s for s in ORDER if s[1] in S_STEPS]
    F_USE = {s: n for n, s in enumerate(F_USES)}
    S_USE = {s: n for n, s in enumerate(S_USES)}
    REST_USES = [[s for s in ORDER if s[1] in k] for k in (("q", "cq"), ("k", "ck"))]
    TR_LAST = {"xT": "v", "cT": "cv", "x1T": "cq", "XT": "o", "cXT": "co"}
    TR_USES = [s for s in ORDER if s[1] in TR_LAST]
    OT_USES = [s for s in ORDER if s[1] in ("pv", "cpv")]

    st = ExitStack()
    with st:
        def sb(name, shape, dt=F32):
            return st.enter_context(nc.sbuf_tensor(name, shape, dt))

        def sem(name):
            return st.enter_context(nc.semaphore(name))

        ident = sb("ident", [P, P])
        identb = sb("identb", [P, P], BF16)
        maskT = sb("maskT", [P, 1, S], BF16)
        wT = sb("wT", [P, 8, P])
        bcol = sb("bcol", [P, NQ])
        brow = sb("brow", [P, 4, E])
        rb_row = sb("rb_row", [P, NEXP])
        hb = sb("hb", [P, NEXP + 1, NF])
        ob = sb("ob", [NEXP + 1, E])
        w1 = sb("w1", [P, NEXP + 1, HID])
        w2 = sb("w2", [P, NEXP + 1, NF, E])
        wr = sb("wr", [P, NEXP])
        tri = sb("tri", [P, NEXP, NEXP])
        epst = sb("epst", [P, NB])
        halfm = sb("halfm", [P, NB])
        RK = sb("RK", [KZ, WPAD], BF16)
        RV = sb("RV", [P, QD, NQ, HD])

        xin = [sb(f"xin{i}", [P, NB, E]) for i in range(2)]
        cin = sb("cin", [P, NB, E])
        TR = [sb(f"TR{i}", [P, T]) for i in range(2)]
        x2T = sb("x2T", [P, T])
        part = [sb(f"part{i}", [P, 3, T], BF16) for i in range(3)]
        rest = [sb(f"rest{i}", [P, T]) for i in range(2)]
        QS = [sb(f"QS{i}", [KD2, HB * S], BF16) for i in range(2)]
        KS = [sb(f"KS{i}", [KD2, HB * S], BF16) for i in range(2)]
        VA = [sb(f"VA{i}", [P, NB, H, HD + 1]) for i in range(2)]
        ST = sb("ST", [P, HB * S])
        PC = sb("PC", [P, NPC, TILE])
        MX = [sb(f"MX{i}", [P, HB * NQ]) for i in range(2)]
        NM = [sb(f"NM{i}", [P, 2, QD]) for i in range(2)]
        NR = [sb(f"NR{i}", [P, 2, QD]) for i in range(2)]
        MP = [sb(f"MP{i}", [P, NSH, 2, QD], BF16) for i in range(2)]
        OT = sb("OT", [P, 2 * BANK])
        OW = sb("OW", [P, H * S])
        X = [sb(f"X{i}", [P, NB, H, HD + 1]) for i in range(2)]
        Y = sb("Y", [P, NB, E])
        acc = sb("acc", [P, NB, E])
        stats = [sb(f"stats{i}", [P, NB, 6]) for i in range(3)]
        mv = [sb(f"mv{i}", [P, NB, 2]) for i in range(3)]
        ve = [sb(f"ve{i}", [P, NB]) for i in range(3)]
        rstd = [sb(f"rstd{i}", [P, NB]) for i in range(3)]
        x1 = sb("x1", [P, NB, E])
        x2 = sb("x2", [P, NB, E])
        lg = sb("lg", [P, NB, NEXP])
        lmax = sb("lmax", [P, NB])
        prob = sb("prob", [P, NB, NEXP])
        lsum = sb("lsum", [P, NB])
        gw = sb("gw", [P, NB, QD])
        gwT = sb("gwT", [NEXP + 1, NB, P])
        HT = [sb(f"HT{i}", [P, NF, T]) for i in range(2)]
        wnat = OT[:, 0:8 * P].rearrange("p (w i) -> p w i", w=8)
        relx = OW[0:HD, 0:WPAD]
        relr = OW[0:HD, WPAD:2 * WPAD]
        relp = OW[0:HD, 2 * WPAD:2 * WPAD + 3 * WPAD // 2].bitcast(BF16).rearrange("d (p w) -> d p w", p=3)
        brows = OW[0:NQ, 4 * WPAD:4 * WPAD + E]
        rv_nat = PC[:, 0, :].rearrange("p (a j d) -> p a j d", a=NQ, j=QD)
        cmp_, cmp2 = (Y[:, 2 * i:2 * i + 2, :].rearrange("p b (r e j) -> p (b r) e j", e=NEXP, j=NEXP) for i in range(2))
        rank = sb("rank", [P, NB, NEXP])

        ps_s = [st.enter_context(nc.psum_tensor(f"ps_s{i}", [P, TILE], F32)) for i in range(2)]
        ps_f = [st.enter_context(nc.psum_tensor(f"ps_f{i}", [P, BANK], F32)) for i in range(4)]

        ld_w = [sem(f"ld_w{i}") for i in range(2)]
        ld_b = sem("ld_b")
        ld_br = sem("ld_br")
        ld_e = sem("ld_e")
        ld_rel = sem("ld_rel")
        ext_done = sem("ext_done")
        ld_rk = sem("ld_rk")
        ld_rv = sem("ld_rv")
        rv_ready = sem("rv_ready")
        ld_x = sem("ld_x")
        ld_c = sem("ld_c")
        c_pool = sem("c_pool")
        zeroed = [sem(f"zeroed{i}") for i in range(2)]
        ones = sem("ones")
        rk_zero = sem("rk_zero")
        c_dve = sem("c_dve")
        rel_step = sem("rel_step")
        wt_ps = sem("wt_ps")
        wt_sb = sem("wt_sb")
        spread_out = {k: sem(f"spread_out_{k}") for k in ("q", "k", "ck", "cq")}
        s_full = sem("s_full")
        f_full = sem("f_full")
        T_ready = {k: sem(f"{k}_ready") for k in ("xT", "x1T", "x2T", "cT", "XT", "cXT")}
        hi_ready = {k: sem(f"hi_{k}") for k in ("q", "k", "ck", "cq")}
        rest_ready = {k: sem(f"rest_{k}") for k in ("q", "k", "ck", "cq")}
        mid_ready = {k: sem(f"mid_{k}") for k in ("q", "k", "ck", "cq")}
        low_ready = {k: sem(f"low_{k}") for k in ("q", "k", "ck", "cq")}
        stacked = {k: sem(f"stacked_{k}") for k in ("q", "k", "ck", "cq")}
        va_ready = [sem(f"va_ready{i}") for i in range(2)]
        bias_ready = sem("bias_ready")
        sum_ready = sem("sum_ready")
        mx_ready = [sem(f"mx_ready{i}") for i in range(2)]
        negmax = [sem(f"negmax{i}") for i in range(2)]
        mp_step = [sem(f"mp_step{i}") for i in range(2)]
        shifted = [sem(f"shifted{i}") for i in range(2)]
        sc_ready = sem("sc_ready")
        ex_ready = sem("ex_ready")
        pr_ready = [sem(f"pr_ready{i}") for i in range(2)]
        ot_ready = [sem(f"ot_ready{i}") for i in range(2)]
        ow_ready = sem("ow_ready")
        xu_ready = [sem(f"xu_ready{i}") for i in range(2)]
        xw_ready = sem("xw_ready")
        rl_ready = [sem(f"rl_ready{i}") for i in range(2)]
        X_ready = [sem(f"X_ready{i}") for i in range(2)]
        res_ready = [sem(f"res_ready{i}") for i in range(2)]
        y_ready = [sem(f"y_ready{i}") for i in range(2)]
        st_ready = [sem(f"st_ready{i}") for i in range(3)]
        mv_ready = [sem(f"mv_ready{i}") for i in range(3)]
        ve_ready = [sem(f"ve_ready{i}") for i in range(3)]
        rstd_ready = [sem(f"rstd_ready{i}") for i in range(3)]
        ln_ready = [sem(f"ln_ready{i}") for i in range(3)]
        r_step = sem("r_step")
        lg_ready = sem("lg_ready")
        exp_ready = sem("exp_ready")
        gw_ready = sem("gw_ready")
        gwT_ready = sem("gwT_ready")
        ht_ready = sem("ht_ready")
        dn_done = sem("dn_done")
        stored = sem("stored")

        AB = {"q": 0, "k": 0, "ck": 1, "cq": 1}

        def released(s):
            ch, what, t = s
            return {
                "xT": lambda: (T_ready["xT"], ch + 1), "x1T": lambda: (T_ready["x1T"], ch + 1),
                "x2T": lambda: (T_ready["x2T"], ch + 1), "cT": lambda: (T_ready["cT"], ch + 1),
                "XT": lambda: (T_ready["XT"], ch + 1), "cXT": lambda: (T_ready["cXT"], ch + 1),
                "q": lambda: (rest_ready["q"], ch + 1), "k": lambda: (rest_ready["k"], ch + 1),
                "ck": lambda: (rest_ready["ck"], ch + 1), "cq": lambda: (rest_ready["cq"], ch + 1),
                "v": lambda: (va_ready[0], ch + 1), "cv": lambda: (va_ready[1], ch + 1),
                "m": lambda: (negmax[0], ch + 1), "cm": lambda: (negmax[1], ch + 1),
                "pv": lambda: (ot_ready[0], NQ * ch + t + 1), "cpv": lambda: (ot_ready[1], NQ * ch + t + 1),
                "w2": lambda: (ow_ready, NQ * ch + t + 1),
                "pvT": lambda: (xu_ready[0], NQ * ch + t + 1), "cpvT": lambda: (xu_ready[1], NQ * ch + t + 1),
                "w2T": lambda: (xw_ready, NQ * ch + t + 1),
                "o": lambda: (y_ready[0], ch + 1), "co": lambda: (y_ready[1], ch + 1),
                "r": lambda: (r_step, R_STEPS * ch + 1), "g": lambda: (gwT_ready, ch + 1),
                "dn": lambda: (dn_done, (NEXP + 1) * ch + t + 1),
                "bias": lambda: (bias_ready, NT * ch + t + 1), "p1": lambda: (mx_ready[0], NT * ch + t + 1),
                "p2": lambda: (sc_ready, NT * ch + t + 1), "c1": lambda: (mx_ready[1], NT * ch + t + 1),
                "c2": lambda: (ex_ready, NT * ch + t + 1), "up": lambda: (ht_ready, (NEXP + 1) * ch + t + 1),
            }[what]()
        R_STEPS = 9

        def take_f(pe, s):
            n = F_USE[s]
            if n >= 4:
                pe.wait_ge(*released(F_USES[n - 4]))
            return ps_f[n % 4]

        def take_s(pe, s):
            n = S_USE[s]
            if n >= 2:
                pe.wait_ge(*released(S_USES[n - 2]))
            return ps_s[n % 2]

        def done_f(e, s):
            e.wait_ge(f_full, F_USE[s] + 1)
            return ps_f[F_USE[s] % 4]

        def transposed(s):
            return TR[TR_USES.index(s) % 2]

        def ot_slot(s):
            return OT_USES.index(s) % 2 * BANK

        def done_s(e, s):
            e.wait_ge(s_full, S_USE[s] + 1)
            return ps_s[S_USE[s] % 2]

        block = st.enter_context(nc.Block())
        N_E = 10
        q_runs, k_runs = runs(Q_PART), runs(K_PART)
        N_RUNS = {"q": len(q_runs), "k": len(k_runs), "ck": len(k_runs), "cq": len(q_runs)}
        SLOT = {"q": 0, "k": 1, "ck": 2, "cq": 3}

        @block.sync
        def _(sp):
            def load_x(ch):
                if ch >= 2:
                    sp.wait_ge(y_ready[0], ch - 1)
                sp.dma_start(xin[ch % 2][:, :, :], xv[ch]).then_inc(ld_x, 16)

            def load_c(ch):
                if ch:
                    done_f(sp, (ch - 1, "cT", 0))
                sp.dma_start(cin[:, :, :], cv[ch]).then_inc(ld_c, 16)

            load_x(0)
            for i, (w, _) in enumerate(sw):
                sp.dma_start(wnat[:, i, :], w).then_inc(ld_w[0], 16)
            sp.dma_start(relx[:, S - 1 - MAX_REL:S + MAX_REL], rel_k.rearrange("r d -> d r"),
                         allow_slow_non_contiguous=True).then_inc(ld_rel, 16)
            for i, (w, _) in enumerate(cw):
                sp.dma_start(wnat[:, 4 + i, :], w).then_inc(ld_w[1], 16)
            load_c(0)
            sp.wait_ge(rel_step, 5)
            sp.wait_ge(rk_zero, 1)
            for c in range(NC):
                sp.dma_start(RK[c * HD:(c + 1) * HD, :], relp[:, K_PART[c], :]).then_inc(ld_rk, 16)

            def load_relative_values():
                n_end = S - 1 - MAX_REL
                sp.dma_start(rel_ext[n_end:S + MAX_REL, :], rel_v).then_inc(ext_done, 16)
                sp.dma_start(rel_ext[0:n_end, :], rel_v[0:1, :].broadcast_to([n_end, HD])).then_inc(ext_done, 16)
                sp.dma_start(rel_ext[S + MAX_REL:WIN, :],
                             rel_v[NREL - 1:NREL, :].broadcast_to([n_end, HD])).then_inc(ext_done, 16)
                sp.wait_ge(ext_done, 48)
                win = bass.AP(rel_ext.tensor, 0, [[HD, P], [HD, S], [1, HD]])
                sp.dma_start(rv_nat.rearrange("p a j d -> p (a j) d"), win).then_inc(ld_rv, 16)

            def load_experts():
                sp.dma_start(rb_row[:, :], router_b.rearrange("(o e) -> o e", o=1).broadcast_to([P, NEXP])).then_inc(ld_e, 16)
                sp.dma_start(hb[:, 0:NEXP, :], rb1.rearrange("e (f p) -> p e f", p=P),
                             allow_slow_non_contiguous=True).then_inc(ld_e, 16)
                sp.dma_start(hb[:, NEXP, :], sb1.rearrange("(f p) -> p f", p=P),
                             allow_slow_non_contiguous=True).then_inc(ld_e, 16)
                sp.dma_start(ob[0:NEXP, :], rb2).then_inc(ld_e, 16)
                sp.dma_start(ob[NEXP:NEXP + 1, :], sb2.rearrange("(o e) -> o e", o=1)).then_inc(ld_e, 16)
                sp.dma_start(w1[:, 0:NEXP, :], rw1.rearrange("e d h -> d e h")).then_inc(ld_e, 16)
                sp.dma_start(w1[:, NEXP, :], sw1).then_inc(ld_e, 16)
                sp.dma_start(w2[:, 0:NEXP, :, :].rearrange("p e f d -> p (e f) d"),
                             rw2.rearrange("e (f p) d -> p (e f) d", p=P)).then_inc(ld_e, 16)
                sp.dma_start(w2[:, NEXP, :, :], sw2.rearrange("(f p) d -> p f d", p=P)).then_inc(ld_e, 16)
                sp.dma_start(wr[:, :], router_w).then_inc(ld_e, 16)

            def spread_parts(ch, what):
                sp.wait_ge(low_ready[what], ch + 1)
                sp.dma_start(spread[4 * ch + SLOT[what]].rearrange("e p t -> p e t"),
                             part[min(SLOT[what], 2)][:, :, :]).then_inc(spread_out[what], 16)

            def stack(ch, what):
                a = AB[what]
                if ch == 0:
                    sp.wait_ge(zeroed[a], 2)
                sp.wait_ge(spread_out[what], 16 * (ch + 1))
                if ch:
                    done_s(sp, (ch - 1, "c2" if a else "p2", NT - 1))
                dst, rr = (QS[a], q_runs) if what in ("q", "cq") else (KS[a], k_runs)
                rows = spread[4 * ch + SLOT[what]].rearrange("e (d h) t -> (e d) (h t)", h=H)
                for c, p, n_ in rr:
                    sp.dma_start(dst[c * HD:(c + n_) * HD, :],
                                 rows[p * HD:(p + n_) * HD, :]).then_inc(stacked[what], 16)

            def shifts(ch, a):
                sp.wait_ge(mp_step[a], 4 * ch + 4)
                for p in range(NSH):
                    dst = QS[a][KZ + p:KZ + p + 1, :].rearrange("o (r c) -> o r c", r=P)
                    sp.dma_start(dst, MP[a][:, p, :, :].rearrange("r f i -> r (f i)")).then_inc(shifted[a], 16)

            for ch, what, t in ORDER:
                if what == "xT" and ch + 1 < NCH:
                    load_x(ch + 1)
                elif what in SLOT:
                    spread_parts(ch, what)
                    if what == "k":
                        stack(ch, "q")
                    if what != "q":
                        stack(ch, what)
                    if ch == 0 and what == "k":
                        load_relative_values()
                        load_experts()
                elif what == "cT" and ch + 1 < NCH:
                    load_c(ch + 1)
                elif what in ("m", "cm"):
                    shifts(ch, int(what == "cm"))
                elif what == "fln":
                    sp.wait_ge(ln_ready[2], ch + 1)
                    sp.dma_start(ov[ch], acc[:, :, :]).then_inc(stored, 16)
            sp.wait_ge(stored, 16 * NCH)

        @block.gpsimd
        def _(g):
            def zeros(a):
                nc.gpsimd.memset(QS[a][0:KD2, :].bitcast(F32), 0.0).then_inc(zeroed[a], 1)
                nc.gpsimd.memset(KS[a][0:KD2, :].bitcast(F32), 0.0).then_inc(zeroed[a], 1)

            nc.gpsimd.memset(ident[:, :], 0.0).then_inc(c_pool, 1)
            g.wait_ge(c_pool, 1)
            nc.gpsimd.affine_select(out=ident[:, :], in_=ident[:, :], compare_op=ALU.not_equal, fill=1.0,
                                    base=0, pattern=[[-1, P]], channel_multiplier=1).then_inc(c_pool, 1)
            nc.gpsimd.memset(RK[0:KZ, :], 0.0).then_inc(rk_zero, 1)
            zeros(0)
            nc.gpsimd.memset(tri[:, :, :], 1.0).then_inc(c_pool, 1)
            nc.gpsimd.memset(epst[:, :], EPS).then_inc(c_pool, 1)
            nc.gpsimd.memset(halfm[:, :], -0.5).then_inc(c_pool, 1)
            nc.gpsimd.memset(maskT[:, :, :], 0.0).then_inc(c_pool, 1)
            g.wait_ge(c_pool, 6)
            nc.gpsimd.affine_select(out=maskT[:, :, :], in_=maskT[:, :, :], compare_op=ALU.is_ge, fill=MASKED,
                                    base=0, pattern=[[0, 1], [1, S]], channel_multiplier=-1).then_inc(c_pool, 1)
            nc.gpsimd.affine_select(out=tri[:, :, :], in_=tri[:, :, :], compare_op=ALU.is_gt, fill=0.0,
                                    base=0, pattern=[[1, NEXP], [-1, NEXP]], channel_multiplier=0).then_inc(c_pool, 1)
            nc.gpsimd.tensor_copy(identb[:, :], ident[:, :]).then_inc(c_pool, 1)
            g.wait_ge(c_pool, 9)
            zeros(1)
            g.wait_ge(ld_br, 16 * 4)

            for ch, what, t in ORDER:
                if what in SLOT:
                    i, r = min(SLOT[what], 2), rest[int(what in ("k", "ck"))]
                    g.wait_ge(rest_ready[what], ch + 1)
                    nc.gpsimd.tensor_copy(part[i][:, 1, :], r[:, :]).then_inc(mid_ready[what], 1)
                    g.wait_ge(mid_ready[what], ch + 1)
                    nc.gpsimd.tensor_tensor(part[i][:, 2, :], r[:, :], part[i][:, 1, :],
                                            ALU.subtract).then_inc(low_ready[what], 1)
                elif what in ("xT", "x1T"):
                    a = int(what == "x1T")
                    r = x1 if a else xin[ch % 2]
                    done_f(g, (ch, what, 0))
                    nc.gpsimd.tensor_tensor(r[:, :, :], r[:, :, :],
                                            brow[:, 2 * a + 1:2 * a + 2, :].broadcast_to([P, NB, E]),
                                            ALU.add).then_inc(res_ready[a], 1)
                elif what == "bias" and ch == 0 and t == 0:
                    g.wait_ge(ld_rv, 16)
                    nc.gpsimd.tensor_copy(RV[:, :, :, :], rv_nat.rearrange("p a j d -> p j a d")).then_inc(rv_ready, 1)
                elif what == "c2":
                    n = NT * ch + t
                    g.wait_ge(ex_ready, n + 1)
                    w = PC[:, n % NPC, :].rearrange("p (g q) -> p g q", q=S)
                    nc.gpsimd.affine_select(out=w, in_=w, compare_op=ALU.is_ge, fill=0.0, base=0,
                                            pattern=[[0, HB_TILE], [1, S]], channel_multiplier=-1).then_inc(pr_ready[1], 1)
                elif what in ("o", "co", "fln"):
                    k = ["o", "co", "fln"].index(what)
                    g.wait_ge(mv_ready[k], ch + 1)
                    nc.gpsimd.tensor_tensor(ve[k][:, :], mv[k][:, :, 1], epst[:, :], ALU.add).then_inc(ve_ready[k], 1)
                    g.wait_ge(ve_ready[k], ch + 1)
                    nc.gpsimd.tensor_tensor(rstd[k][:, :], ve[k][:, :], halfm[:, :], ALU.pow).then_inc(rstd_ready[k], 1)

        @block.tensor
        def _(pe):
            pe.wait_ge(c_pool, 2)
            for i in range(8):
                if i % 4 == 0:
                    pe.wait_ge(ld_w[i // 4], 16 * 4)
                nc.tensor.transpose(ps_s[i // 4][:, (i % 4) * P:(i % 4 + 1) * P], wnat[:, i, :],
                                    ident[:, :]).then_inc(wt_ps, 1)
                if i == 3:
                    pe.wait_ge(ld_b, 16 * 4)
                    nc.tensor.transpose(ps_f[3][:, 0:NQ], brows, ident[0:NQ, 0:NQ]).then_inc(wt_ps, 1)
            pe.wait_ge(wt_sb, 5)
            pe.wait_ge(c_dve, 5)

            def transposes(s, src):
                ps = take_f(pe, s)
                for b in range(NB):
                    last = nc.tensor.transpose(ps[:, b * S:(b + 1) * S], src(b), ident[:, :])
                last.then_inc(f_full, 1)

            def project(s, w, src):
                ps = take_f(pe, s)
                nc.tensor.matmul(ps[:, :], wT[:, w, :], src[:, :], start=True, stop=True).then_inc(f_full, 1)

            def rows(s, w, src):
                ps = take_f(pe, s)
                for b in range(NB):
                    last = nc.tensor.matmul(ps[:, b * E:(b + 1) * E], src[:, b * S:(b + 1) * S], wT[:, w, :],
                                            start=True, stop=True)
                last.then_inc(f_full, 1)

            def scores(s, a, kd, masked):
                ps, t = take_s(pe, s), s[2]
                for half in range(2):
                    if masked:
                        nc.tensor.matmul(ps[:, half * BANK:(half + 1) * BANK], identb[:, :],
                                         maskT[:, :, :].broadcast_to([P, 4, S]), start=True, stop=False,
                                         skip_group_check=True)
                    for j in range(4):
                        c = (t * HB_TILE + half * 4 + j) * S
                        o = (half * 4 + j) * S
                        last = nc.tensor.matmul(ps[:, o:o + S], KS[a][0:kd, c:c + S], QS[a][0:kd, c:c + S],
                                                start=not masked and j == 0, stop=j == 3, skip_group_check=True)
                last.then_inc(s_full, 1)

            def maxima(s, a):
                pe.wait_ge(mx_ready[a], NT * (s[0] + 1))
                ps = take_f(pe, s)
                for f in range(2):
                    last = nc.tensor.transpose(ps[:, f * P:(f + 1) * P],
                                               MX[a][:, :].rearrange("p (r f) -> p f r", f=2)[:, f, :], ident[:, :])
                last.then_inc(f_full, 1)

            def values(s, a, prob_of):
                ps = take_f(pe, s)
                for j in range(HQ):
                    for b in range(NB):
                        h = HQ * s[2] + j
                        last = nc.tensor.matmul(ps[b * QD:b * QD + HD + 1, j * S:(j + 1) * S], VA[a][:, b, h, :],
                                                prob_of(h, b), start=j == 0, stop=j == HQ - 1,
                                                tile_position=(0, b * QD), skip_group_check=True)
                last.then_inc(f_full, 1)

            def to_tokens(s, src):
                ps = take_f(pe, s)
                for j in range(HQ):
                    last = nc.tensor.transpose(ps[:, j * P:(j + 1) * P], src(HQ * s[2] + j), ident[:, :])
                last.then_inc(f_full, 1)

            qs_q = QS[0][0:KZ, :].rearrange("k (g q) -> k g q", q=S)
            st_q = ST[:, :].rearrange("p (h b a j) -> p h b a j", h=H, b=NB, a=NQ)
            st_h = ST[:, :].rearrange("p (h b q) -> p h b q", h=H, b=NB)
            pc_h = PC[:, :, :].rearrange("p t (g b q) -> p t g b q", b=NB, q=S)

            for s in ORDER:
                ch, what, t = s
                if what == "xT":
                    pe.wait_ge(ld_x, 16 * (ch + 1))
                    transposes(s, lambda b: xin[ch % 2][:, b, :])
                elif what == "cT":
                    pe.wait_ge(ld_c, 16 * (ch + 1))
                    transposes(s, lambda b: cin[:, b, :])
                elif what == "x1T":
                    pe.wait_ge(ln_ready[0], ch + 1)
                    transposes(s, lambda b: x1[:, b, :])
                elif what == "x2T":
                    pe.wait_ge(ln_ready[1], ch + 1)
                    transposes(s, lambda b: x2[:, b, :])
                elif what in ("q", "k", "v"):
                    pe.wait_ge(T_ready["xT"], ch + 1)
                    if what == "v":
                        rows(s, 2, transposed((ch, "xT", 0)))
                    else:
                        project(s, "qk".index(what), transposed((ch, "xT", 0)))
                elif what in ("ck", "cv"):
                    pe.wait_ge(T_ready["cT"], ch + 1)
                    if what == "ck":
                        project(s, 5, transposed((ch, "cT", 0)))
                    else:
                        rows(s, 6, transposed((ch, "cT", 0)))
                elif what == "cq":
                    pe.wait_ge(T_ready["x1T"], ch + 1)
                    project(s, 4, transposed((ch, "x1T", 0)))
                elif what == "bias":
                    if t == 0:
                        pe.wait_ge(stacked["q"], 16 * N_RUNS["q"] * (ch + 1))
                        pe.wait_ge(ld_rk, 16 * NC)
                    ps = take_s(pe, s)
                    for j in range(S // NT):
                        q = t * (S // NT) + j
                        last = nc.tensor.matmul(ps[:, j * HB:(j + 1) * HB], RK[:, S - 1 - q:2 * S - 1 - q],
                                                qs_q[:, :, q], start=True, stop=True)
                    last.then_inc(s_full, 1)
                elif what == "p1":
                    if t == 0:
                        pe.wait_ge(ones, 1)
                        pe.wait_ge(stacked["k"], 16 * N_RUNS["k"] * (ch + 1))
                    scores(s, 0, KZ, False)
                elif what in ("m", "cm"):
                    maxima(s, int(what == "cm"))
                elif what == "p2":
                    if t == 0:
                        pe.wait_ge(ones, 1)
                        pe.wait_ge(shifted[0], 16 * NSH * (ch + 1))
                    scores(s, 0, KD2, False)
                elif what == "c1":
                    if t == 0:
                        pe.wait_ge(ones, 2)
                        pe.wait_ge(c_pool, 9)
                        pe.wait_ge(stacked["ck"], 16 * N_RUNS["ck"] * (ch + 1))
                        pe.wait_ge(stacked["cq"], 16 * N_RUNS["cq"] * (ch + 1))
                    scores(s, 1, KZ, True)
                elif what == "c2":
                    if t == 0:
                        pe.wait_ge(shifted[1], 16 * NSH * (ch + 1))
                    scores(s, 1, KD2, False)
                elif what in ("pv", "cpv"):
                    a = int(what == "cpv")
                    pe.wait_ge(va_ready[a], ch + 1)
                    pe.wait_ge(pr_ready[a], NT * ch + 2 * t + 2)
                    values(s, a, (lambda h, b: pc_h[:, (NT * ch + h // 2) % NPC, h % 2, b, :]) if a else (lambda h, b: st_h[:, h, b, :]))
                elif what == "w2":
                    pe.wait_ge(pr_ready[0], NT * (ch + 1))
                    if t == 0:
                        pe.wait_ge(rv_ready, 1)
                    ps = take_f(pe, s)
                    for jj in range(QD // NQ):
                        j = t * (QD // NQ) + jj
                        for b in range(NB):
                            last = nc.tensor.matmul(ps[b * QD:(b + 1) * QD, jj * HB:(jj + 1) * HB],
                                                    RV[:, QD - 1 - j, :, :].rearrange("p a d -> p (a d)"),
                                                    st_q[:, :, b, :, j].rearrange("p h a -> p a h"),
                                                    start=jj == 0, stop=jj == QD // NQ - 1,
                                                    tile_position=(0, b * QD), skip_group_check=True)
                    last.then_inc(f_full, 1)
                elif what in ("pvT", "cpvT"):
                    pe.wait_ge(ot_ready[int(what == "cpvT")], NQ * ch + t + 1)
                    o = ot_slot((ch, what[:-1], t))
                    to_tokens(s, lambda h: OT[:, o + h % HQ * S:o + (h % HQ + 1) * S])
                elif what == "w2T":
                    pe.wait_ge(ow_ready, NQ * (ch + 1))
                    to_tokens(s, lambda h: OW[:, h * S:(h + 1) * S])
                elif what in ("XT", "cXT"):
                    a = int(what == "cXT")
                    pe.wait_ge(X_ready[a], ch + 1)
                    transposes(s, lambda b: Y[:, b, :])
                elif what in ("o", "co"):
                    a = int(what == "co")
                    pe.wait_ge(T_ready["cXT" if a else "XT"], ch + 1)
                    rows(s, 4 * a + 3, transposed((ch, "cXT" if a else "XT", 0)))
                elif what == "r":
                    pe.wait_ge(T_ready["x2T"], ch + 1)
                    pe.wait_ge(ld_e, 16 * N_E)
                    ps = take_f(pe, s)
                    for b in range(NB):
                        last = nc.tensor.matmul(ps[:, b * NEXP:(b + 1) * NEXP], x2T[:, b * S:(b + 1) * S], wr[:, :],
                                                start=True, stop=True)
                    last.then_inc(f_full, 1)
                elif what == "g":
                    pe.wait_ge(gw_ready, ch + 1)
                    ps = take_f(pe, s)
                    for b in range(NB):
                        last = nc.tensor.transpose(ps[0:QD, b * S:(b + 1) * S], gw[:, b, :], ident[:, :])
                    last.then_inc(f_full, 1)
                elif what == "up":
                    e = (t - 1) % (NEXP + 1)
                    ps = take_s(pe, s)
                    for f in range(NF):
                        last = nc.tensor.matmul(ps[:, f * T:(f + 1) * T], w1[:, e, f * P:(f + 1) * P], x2T[:, :],
                                                start=True, stop=True)
                    last.then_inc(s_full, 1)
                elif what == "dn":
                    e = (t - 1) % (NEXP + 1)
                    n = ch * (NEXP + 1) + t
                    pe.wait_ge(ht_ready, n + 1)
                    if t == 0:
                        pe.wait_ge(gwT_ready, ch + 1)
                    ps = take_f(pe, s)
                    for b in range(NB):
                        for f in range(NF):
                            last = nc.tensor.matmul(ps[:, b * E:(b + 1) * E], HT[n % 2][:, f, b * S:(b + 1) * S],
                                                    w2[:, e, f, :], start=f == 0, stop=f == NF - 1 and t > 0)
                        if t == 0:
                            last = nc.tensor.matmul(ps[:, b * E:(b + 1) * E], gwT[:, b, :], ob[:, :],
                                                    start=False, stop=True)
                    last.then_inc(f_full, 1)

        @block.scalar
        def _(act):
            for i, b in enumerate([sw[0][1], sw[1][1], cw[0][1], cw[1][1]]):
                nc.scalar.dma_start(brows[i:i + 1, :].rearrange("o (d h) -> o d h", h=H),
                                    b.rearrange("(o h d) -> o d h", o=1, h=H), allow_slow_non_contiguous=True).then_inc(ld_b, 16)
            for i, b in enumerate([sw[2][1], sw[3][1], cw[2][1], cw[3][1]]):
                nc.scalar.dma_start(brow[:, i, :], b.rearrange("(o e) -> o e", o=1).broadcast_to([P, E])).then_inc(ld_br, 16)
            for i in range(2):
                act.wait_ge(wt_ps, 5 * i + 4)
                src = ps_s[i][:, 0:BANK].rearrange("p (w o) -> p w o", w=4)
                nc.scalar.copy(wT[:, 4 * i:4 * i + 2, :].rearrange("p w (d h) -> p w d h", h=H),
                               src[:, 0:2, :].rearrange("p w (h d) -> p w d h", h=H)).then_inc(wt_sb, 1)
                nc.scalar.copy(wT[:, 4 * i + 2:4 * i + 4, :], src[:, 2:4, :]).then_inc(wt_sb, 1)
                if i == 0:
                    act.wait_ge(wt_ps, 5)
                    nc.scalar.copy(bcol[:, :], ps_f[3][:, 0:NQ]).then_inc(wt_sb, 1)
            act.wait_ge(wt_sb, 5)

            for s in ORDER:
                ch, what, t = s
                if what in ("xT", "x1T", "x2T", "cT", "XT", "cXT"):
                    dst = x2T if what == "x2T" else transposed(s)
                    ps = done_f(act, s)
                    if what == "x2T" and ch:
                        done_s(act, (ch - 1, "up", NEXP))
                    if what != "x2T" and TR_USES.index(s) >= 2:
                        c_, w_, _ = TR_USES[TR_USES.index(s) - 2]
                        done_f(act, (c_, TR_LAST[w_], 0))
                    nc.scalar.copy(dst[:, :], ps[:, :]).then_inc(T_ready[what], 1)
                elif what in SLOT:
                    ps = done_f(act, s)
                    i = min(SLOT[what], 2)
                    if what == "cq":
                        act.wait_ge(stacked["ck"], 16 * N_RUNS["ck"] * (ch + 1))
                    elif ch:
                        k = {"q": "q", "k": "k", "ck": "cq"}[what]
                        act.wait_ge(stacked[k], 16 * N_RUNS[k] * ch)
                    b = ["q", "k", "cq", "ck"].index(what)
                    nc.scalar.activation(part[i][:, 0, :], ps[:, :], ACT.Identity, bias=bcol[:, b:b + 1]).then_inc(hi_ready[what], 1)
                elif what == "bias":
                    ps = done_s(act, s)
                    if t == 0 and ch:
                        done_f(act, (ch - 1, "w2", NQ - 1))
                    nq = S // NT
                    dst = ST[:, :].rearrange("p (g q) -> p g q", q=S)[:, :, t * nq:(t + 1) * nq]
                    nc.scalar.copy(dst, ps[:, :].rearrange("p (q g) -> p g q", g=HB)).then_inc(bias_ready, 1)
                elif what == "p2":
                    act.wait_ge(sc_ready, NT * ch + t + 1)
                    w = ST[:, t * TILE:(t + 1) * TILE]
                    nc.scalar.activation(w, w, ACT.Exp, scale=SCALE).then_inc(pr_ready[0], 1)
                elif what == "c2":
                    ps = done_s(act, s)
                    n = NT * ch + t
                    if n == 0:
                        act.wait_ge(rv_ready, 1)
                    if n >= NPC:
                        c_, t_ = divmod(n - NPC, NT)
                        done_f(act, (c_, "cpv", t_ // 2))
                    nc.scalar.activation(PC[:, n % NPC, :], ps[:, :], ACT.Exp, scale=SCALE).then_inc(ex_ready, 1)
                elif what in ("pv", "cpv"):
                    ps = done_f(act, s)
                    n = OT_USES.index(s)
                    if n >= 2:
                        c_, w_, t_ = OT_USES[n - 2]
                        done_f(act, (c_, w_ + "T", t_))
                    o = ot_slot(s)
                    nc.scalar.copy(OT[:, o:o + BANK], ps[:, :]).then_inc(ot_ready[int(what == "cpv")], 1)
                elif what == "w2":
                    ps = done_f(act, s)
                    if ch:
                        done_f(act, (ch - 1, "w2T", NQ - 1))
                    nj = QD // NQ
                    nc.scalar.copy(OW[:, :].rearrange("p (h a j) -> p h a j", h=H, a=NQ)[:, :, :, t * nj:(t + 1) * nj],
                                   ps[:, :].rearrange("p (j a h) -> p h a j", j=nj, a=NQ)).then_inc(ow_ready, 1)
                elif what in ("pvT", "cpvT"):
                    a = int(what == "cpvT")
                    ps = done_f(act, s)
                    if ch:
                        act.wait_ge(X_ready[a], ch)
                    nc.scalar.copy(X[a][:, :, HQ * t:HQ * (t + 1), :].rearrange("p b h d -> p h b d"),
                                   ps[:, :].rearrange("p (h b d) -> p h b d", h=HQ, b=NB)[:, :, :, 0:HD + 1]
                                   ).then_inc(xu_ready[a], 1)
                elif what == "r":
                    act.wait_ge(lg_ready, ch + 1)
                    nc.scalar.activation(prob[:, :, :], lg[:, :, :], ACT.Exp).then_inc(exp_ready, 1)
                elif what == "up":
                    e = (t - 1) % (NEXP + 1)
                    n = ch * (NEXP + 1) + t
                    ps = done_s(act, s)
                    if n >= 2:
                        c_, t_ = divmod(n - 2, NEXP + 1)
                        done_f(act, (c_, "dn", t_))
                    for f in range(NF):
                        last = nc.scalar.activation(HT[n % 2][:, f, :], ps[:, f * T:(f + 1) * T], ACT.Gelu,
                                                    bias=hb[:, e, f:f + 1])
                    last.then_inc(ht_ready, 1)

        @block.vector
        def _(v):
            def one_rows(a):
                v.wait_ge(zeroed[a], 2)
                nc.vector.memset(KS[a][64:KD2, :].bitcast(F32), TWO_ONES).then_inc(ones, 1)

            v.wait_ge(ld_rel, 16)
            n_end = S - 1 - MAX_REL
            nc.vector.tensor_copy(relx[:, 0:n_end], relx[:, n_end:n_end + 1].broadcast_to([HD, n_end]))
            nc.vector.tensor_copy(relx[:, S + MAX_REL:WPAD],
                                  relx[:, S + MAX_REL - 1:S + MAX_REL].broadcast_to([HD, WPAD - S - MAX_REL])).then_inc(rel_step, 1)
            v.wait_ge(rel_step, 1)
            nc.vector.tensor_copy(relp[:, 0, :], relx).then_inc(rel_step, 1)
            v.wait_ge(rel_step, 2)
            nc.vector.tensor_tensor(relr, relx, relp[:, 0, :], ALU.subtract).then_inc(rel_step, 1)
            v.wait_ge(rel_step, 3)
            nc.vector.tensor_copy(relp[:, 1, :], relr).then_inc(rel_step, 1)
            v.wait_ge(rel_step, 4)
            nc.vector.tensor_tensor(relp[:, 2, :], relr, relp[:, 1, :], ALU.subtract).then_inc(rel_step, 1)
            for a in range(2):
                nc.vector.memset(VA[a][:, :, :, HD:HD + 1], 1.0).then_inc(c_dve, 1)
            nc.vector.memset(gw[:, :, :], 0.0).then_inc(c_dve, 1)
            v.wait_ge(c_dve, 3)
            nc.vector.memset(gw[:, :, NEXP:NEXP + 1], 1.0).then_inc(c_dve, 1)
            for i in range(4):
                if i == 3:
                    v.wait_ge(wt_sb, 3)
                last = nc.vector.memset(ps_f[i][:, :], 0.0)
            last.then_inc(c_dve, 1)
            v.wait_ge(ld_br, 16 * 4)

            def flat(a):
                return a[:, :, :].rearrange("p b e -> p (b e)")

            def statistics(k, ch, y):
                for b in range(NB):
                    last = nc.vector.bn_stats(stats[k][:, b, :], y[:, b, :])
                last.then_inc(st_ready[k], 1)
                v.wait_ge(st_ready[k], ch + 1)
                for b in range(NB):
                    last = nc.vector.bn_aggr(mv[k][:, b, :], stats[k][:, b, :])
                last.then_inc(mv_ready[k], 1)

            def normalise(k, ch, y, o):
                v.wait_ge(rstd_ready[k], ch + 1)
                for b in range(NB):
                    last = nc.vector.tensor_scalar(o[:, b, :], y[:, b, :], mv[k][:, b, 0:1], rstd[k][:, b:b + 1],
                                                   ALU.subtract, ALU.mult)
                last.then_inc(ln_ready[k], 1)

            for s in ORDER:
                ch, what, t = s
                if what in SLOT:
                    ps = done_f(v, s)
                    i = min(SLOT[what], 2)
                    v.wait_ge(hi_ready[what], ch + 1)
                    k = int(what in ("k", "ck"))
                    n = REST_USES[k].index(s)
                    if n:
                        v.wait_ge(low_ready[REST_USES[k][n - 1][1]], REST_USES[k][n - 1][0] + 1)
                    b = ["q", "k", "cq", "ck"].index(what)
                    nc.vector.scalar_tensor_tensor(rest[k][:, :], ps[:, :], bcol[:, b:b + 1], part[i][:, 0, :],
                                                   ALU.add, ALU.subtract).then_inc(rest_ready[what], 1)
                elif what in ("v", "cv"):
                    a = int(what == "cv")
                    if ch == 0:
                        one_rows(a)
                    ps = done_f(v, s)
                    if ch:
                        done_f(v, (ch - 1, "cpv" if a else "pv", NQ - 1))
                    nc.vector.tensor_tensor(VA[a][:, :, :, 0:HD],
                                            ps[:, :].rearrange("p (b h d) -> p b h d", b=NB, h=H),
                                            brow[:, 2 * a:2 * a + 1, :].rearrange("p o (h d) -> p o h d", h=H)
                                            .broadcast_to([P, NB, H, HD]), ALU.add).then_inc(va_ready[a], 1)
                elif what == "p1":
                    ps = done_s(v, s)
                    if t == 0:
                        v.wait_ge(bias_ready, NT * (ch + 1))
                    nc.vector.tensor_tensor(ps[:, :], ps[:, :], ST[:, t * TILE:(t + 1) * TILE],
                                            ALU.add).then_inc(sum_ready, 1)
                    v.wait_ge(sum_ready, NT * ch + t + 1)
                    nc.vector.tensor_reduce(MX[0][:, t * 32:(t + 1) * 32], ps[:, :].rearrange("p (c i) -> p c i", i=QD),
                                            AXIS.X, ALU.max, apply_transpose=True).then_inc(mx_ready[0], 1)
                elif what == "c1":
                    ps = done_s(v, s)
                    nc.vector.tensor_reduce(MX[1][:, t * 32:(t + 1) * 32], ps[:, :].rearrange("p (c i) -> p c i", i=QD),
                                            AXIS.X, ALU.max, apply_transpose=True).then_inc(mx_ready[1], 1)
                elif what in ("m", "cm"):
                    a = int(what == "cm")
                    ps = done_f(v, s)
                    nc.vector.tensor_reduce(NM[a][:, :, :], ps[:, 0:2 * P].rearrange("p (f a i) -> p f i a", f=2, a=NQ),
                                            AXIS.X, ALU.max, negate=True).then_inc(negmax[a], 1)
                    v.wait_ge(negmax[a], ch + 1)
                    if ch:
                        v.wait_ge(shifted[a], 16 * NSH * ch)
                    nc.vector.tensor_copy(MP[a][:, 0, :, :], NM[a][:, :, :]).then_inc(mp_step[a], 1)
                    v.wait_ge(mp_step[a], 4 * ch + 1)
                    nc.vector.tensor_tensor(NR[a][:, :, :], NM[a][:, :, :], MP[a][:, 0, :, :], ALU.subtract).then_inc(mp_step[a], 1)
                    v.wait_ge(mp_step[a], 4 * ch + 2)
                    nc.vector.tensor_copy(MP[a][:, 1, :, :], NR[a][:, :, :]).then_inc(mp_step[a], 1)
                    v.wait_ge(mp_step[a], 4 * ch + 3)
                    nc.vector.tensor_tensor(MP[a][:, 2, :, :], NR[a][:, :, :], MP[a][:, 1, :, :], ALU.subtract).then_inc(mp_step[a], 1)
                elif what == "p2":
                    ps = done_s(v, s)
                    w = ST[:, t * TILE:(t + 1) * TILE]
                    nc.vector.tensor_tensor(w, ps[:, :], w, ALU.add).then_inc(sc_ready, 1)
                elif what == "w2T":
                    ps = done_f(v, s)
                    v.wait_ge(xu_ready[0], NQ * (ch + 1))
                    o = ps[:, :].rearrange("p (h b a d) -> p h b a d", h=HQ, b=NB, a=NQ)
                    for a in range(NQ):
                        r = slice(a * QD, (a + 1) * QD)
                        xo = X[0][r, :, HQ * t:HQ * (t + 1), 0:HD].rearrange("p b h d -> p h b d")
                        last = nc.vector.tensor_tensor(xo, o[r, :, :, NQ - 1 - a, :], xo, ALU.add)
                    last.then_inc(xw_ready, 1)
                elif what in ("X", "cX"):
                    a = int(what == "cX")
                    v.wait_ge(xu_ready[a], NQ * (ch + 1))
                    if not a:
                        v.wait_ge(xw_ready, NQ * (ch + 1))
                    den = X[a][:, :, :, HD:HD + 1]
                    nc.vector.reciprocal(den, den).then_inc(rl_ready[a], 1)
                    v.wait_ge(rl_ready[a], ch + 1)
                    nc.vector.tensor_tensor(Y[:, :, :].rearrange("p b (h d) -> p b h d", h=H), X[a][:, :, :, 0:HD], den.broadcast_to([P, NB, H, HD]), ALU.mult).then_inc(X_ready[a], 1)
                elif what in ("o", "co"):
                    a = int(what == "co")
                    ps = done_f(v, s)
                    v.wait_ge(res_ready[a], ch + 1)
                    nc.vector.tensor_tensor(flat(Y), ps[:, :], flat(x1 if a else xin[ch % 2]), ALU.add).then_inc(y_ready[a], 1)
                    v.wait_ge(y_ready[a], ch + 1)
                    statistics(a, ch, Y)
                elif what == "ln":
                    normalise(0, ch, Y, x1)
                elif what == "cln":
                    normalise(1, ch, Y, x2)
                elif what == "r":
                    ps = done_f(v, s)
                    if ch == 0:
                        v.wait_ge(ld_e, 16 * N_E)
                        v.wait_ge(c_pool, 9)
                    nc.vector.tensor_tensor(lg[:, :, :], ps[:, 0:NB * NEXP].rearrange("p (b e) -> p b e", b=NB),
                                            rb_row[:, :].rearrange("p (o e) -> p o e", o=1).broadcast_to([P, NB, NEXP]),
                                            ALU.add).then_inc(r_step, 1)
                    r = R_STEPS * ch
                    v.wait_ge(r_step, r + 1)
                    nc.vector.tensor_reduce(lmax[:, :], lg[:, :, :], AXIS.X, ALU.max).then_inc(r_step, 1)
                    v.wait_ge(r_step, r + 2)

                    def over(a):
                        return a[:, :].rearrange("p (b o) -> p b o", o=1).broadcast_to([P, NB, NEXP])
                    nc.vector.tensor_tensor(lg[:, :, :], lg[:, :, :], over(lmax), ALU.subtract).then_inc(lg_ready, 1)
                    v.wait_ge(exp_ready, ch + 1)
                    nc.vector.tensor_reduce(lsum[:, :], prob[:, :, :], AXIS.X, ALU.add).then_inc(r_step, 1)
                    v.wait_ge(r_step, r + 3)
                    nc.vector.reciprocal(lmax[:, :], lsum[:, :]).then_inc(r_step, 1)
                    v.wait_ge(r_step, r + 4)
                    nc.vector.tensor_tensor(prob[:, :, :], prob[:, :, :], over(lmax), ALU.mult).then_inc(r_step, 1)
                    v.wait_ge(r_step, r + 5)
                    pj = prob[:, :, :].rearrange("p b (o j) -> p b o j", o=1).broadcast_to([P, NB, NEXP, NEXP])
                    pi = prob[:, :, :].rearrange("p b (e o) -> p b e o", o=1).broadcast_to([P, NB, NEXP, NEXP])
                    nc.vector.tensor_tensor(cmp_[:, :, :, :], pj, pi, ALU.is_gt)
                    nc.vector.tensor_tensor(cmp2[:, :, :, :], pj, pi, ALU.is_equal).then_inc(r_step, 1)
                    v.wait_ge(r_step, r + 6)
                    tb = tri[:, :, :].rearrange("p (o e) j -> p o e j", o=1).broadcast_to([P, NB, NEXP, NEXP])
                    nc.vector.tensor_tensor(cmp2[:, :, :, :], cmp2[:, :, :, :], tb, ALU.mult).then_inc(r_step, 1)
                    v.wait_ge(r_step, r + 7)
                    nc.vector.tensor_tensor(cmp_[:, :, :, :], cmp_[:, :, :, :], cmp2[:, :, :, :], ALU.add).then_inc(r_step, 1)
                    v.wait_ge(r_step, r + 8)
                    nc.vector.tensor_reduce(rank[:, :, :], cmp_[:, :, :, :], AXIS.X, ALU.add).then_inc(r_step, 1)
                    v.wait_ge(r_step, r + 9)
                    nc.vector.scalar_tensor_tensor(gw[:, :, 0:NEXP], rank[:, :, :], float(TOP_K), prob[:, :, :],
                                                   ALU.is_lt, ALU.mult).then_inc(gw_ready, 1)
                elif what == "g":
                    ps = done_f(v, s)
                    nc.vector.tensor_copy(gwT[:, :, :].rearrange("p b t -> p (b t)"), ps[0:NEXP + 1, :]).then_inc(gwT_ready, 1)
                elif what == "dn":
                    n = ch * (NEXP + 1) + t
                    ps = done_f(v, s)
                    if t == 0:
                        if ch:
                            v.wait_ge(stored, 16 * ch)
                        nc.vector.tensor_tensor(flat(acc), ps[:, :], flat(x2), ALU.add).then_inc(dn_done, 1)
                    else:
                        v.wait_ge(dn_done, n)
                        for b in range(NB):
                            last = nc.vector.scalar_tensor_tensor(acc[:, b, :], ps[:, b * E:(b + 1) * E],
                                                                  gw[:, b, t - 1:t], acc[:, b, :], ALU.mult, ALU.add)
                        last.then_inc(dn_done, 1)
                elif what == "fln":
                    v.wait_ge(dn_done, (ch + 1) * (NEXP + 1))
                    statistics(2, ch, acc)
                    normalise(2, ch, acc, acc)


_ATTN = ["Wq", "bq", "Wk", "bk", "Wv", "bv", "Wo", "bo"]
_INS = (["x", "ctx_1024"] + [f"L0_attn_{n}" for n in _ATTN] + ["L0_attn_rel_k", "L0_attn_rel_v"]
        + [f"L0_xattn_{n}" for n in _ATTN]
        + [f"L0_ffn_{n}" for n in ["router_w", "router_b", "sw1", "sb1", "sw2", "sb2", "rw1", "rb1", "rw2", "rb2"]])


def kernel(**inputs):
    import numpy as np
    import concourse.bacc as bacc
    from concourse.bass_utils import run_bass_kernel_spmd as run

    nc = bacc.Bacc("TRN2", target_bir_lowering=False, num_devices=1)
    arrays, ap = {}, {}
    for name in _INS:
        a = np.ascontiguousarray(inputs[name])
        arrays[f"in_{name}"] = a
        ap[name] = nc.dram_tensor(f"in_{name}", a.shape, mybir.dt.from_np(a.dtype), kind="ExternalInput").ap()
    shape = inputs["x"].shape
    out = nc.dram_tensor("out_x", shape, mybir.dt.float32, kind="ExternalOutput").ap()
    rel_ext = nc.dram_tensor("rel_v_by_distance", (WIN, HD), mybir.dt.float32, kind="Internal").ap()
    spread = nc.dram_tensor("parts_by_head", (4 * (shape[0] // NB), 3, E, T), mybir.dt.bfloat16, kind="Internal").ap()

    def layer(p):
        return [(ap[f"{p}_W{n}"], ap[f"{p}_b{n}"]) for n in "qkvo"]
    f = {n[7:]: a for n, a in ap.items() if n.startswith("L0_ffn_")}
    build(nc, ap["x"], ap["ctx_1024"], layer("L0_attn"), layer("L0_xattn"), ap["L0_attn_rel_k"],
          ap["L0_attn_rel_v"], f["router_w"], f["router_b"], f["sw1"], f["sb1"], f["sw2"], f["sb2"],
          f["rw1"], f["rb1"], f["rw2"], f["rb2"], rel_ext, spread, out)
    r = run(nc, [arrays], core_ids=[0])
    return r.results[0]["out_x"]
```

```python
import concourse.bass as bass
from concourse import mybir
from contextlib import ExitStack

F32 = mybir.dt.float32
BF16 = mybir.dt.bfloat16
U32 = mybir.dt.uint32
ACT = mybir.ActivationFunctionType
ALU = mybir.AluOpType
AXIS = mybir.AxisListType

P = 128
S = 128
E = 128
H = 16
HD = E // H
MAX_REL = 20
NREL = 2 * MAX_REL + 1
NB = 4
T = NB * S
HB = H * NB
HB_TILE = 8
TILE = HB_TILE * S
NT = HB // HB_TILE
BANK = 512
NQ = 4
QD = P // NQ
HQ = H // NQ
NEXP = 8
TOP_K = 2
HID = 256
NF = HID // P
NPC = 3
WIN = 2 * S - 1
WPAD = 256
EPS = 1e-5
TWO_ONES = 1.0019378662109375
SCALE = float(HD) ** -0.5
MASKED = -1.0e30

Q_PART = [0, 1, 2, 0, 1, 0]
K_PART = [0, 1, 0, 1, 0, 2]
NC = len(Q_PART)
KD = NC * HD
KZ = 65
NSH = 3
KD2 = KZ + NSH


def runs(parts):
    out = []
    for c, p in enumerate(parts):
        if out and out[-1][1] + out[-1][2] == p and out[-1][0] + out[-1][2] == c:
            out[-1][2] += 1
        else:
            out.append([c, p, 1])
    return out


CHUNK_AT = [0.00, 96.37, 192.71, 289.19]
PLACE = {
    "xT": (1, 0.00, 0.000),
    "q": (1, 4.33, 0.000),
    "v": (1, 4.66, 0.000),
    "k": (1, 5.82, 0.000),
    "bias": (NT, 23.17, 0.050),
    "p1": (NT, 24.76, 4.292),
    "cT": (1, 42.77, 0.000),
    "m": (2, 48.47, 7.457),
    "p2": (NT, 59.45, 1.603),
    "pv": (NQ, 67.85, 3.199),
    "cv": (1, 69.86, 0.000),
    "pvT": (NQ, 75.23, 6.017),
    "ck": (1, 76.77, 0.000),
    "w2": (NQ, 77.85, 4.573),
    "w2T": (NQ, 94.43, 1.175),
    "X": (1, 98.44, 0.000),
    "XT": (1, 101.40, 0.000),
    "o": (1, 101.89, 0.000),
    "ln": (1, 106.01, 0.000),
    "x1T": (1, 112.00, 0.000),
    "cq": (1, 113.67, 0.000),
    "c1": (NT, 137.48, 0.626),
    "cm": (2, 140.38, 4.415),
    "c2": (NT, 143.66, 1.573),
    "cpv": (NQ, 148.79, 3.459),
    "cpvT": (NQ, 155.64, 2.366),
    "cX": (1, 164.03, 0.000),
    "cXT": (1, 166.46, 0.000),
    "co": (1, 171.02, 0.000),
    "cln": (1, 177.53, 0.000),
    "x2T": (1, 182.61, 0.000),
    "r": (1, 183.56, 0.000),
    "up": ((NEXP + 1) * NF, 187.71, 2.957),
    "g": (1, 196.47, 0.000),
    "dn": (NEXP + 1, 198.21, 5.957),
    "fln": (1, 249.01, 0.000),
}
F_STEPS = {"xT", "q", "k", "v", "m", "pv", "w2", "pvT", "w2T", "XT", "o", "cT", "ck", "cv", "x1T", "cq", "cm",
           "cpv", "cpvT", "cXT", "co", "x2T", "r", "g", "up", "dn"}
S_STEPS = {"bias", "p1", "p2", "c1", "c2"}


def build(nc, x, ctx, sw, cw, rel_k, rel_v, router_w, router_b, sw1, sb1, sw2, sb2,
          rw1, rb1, rw2, rb2, rel_ext, spread, out):
    NCH = x.shape[0] // NB
    xv = x.rearrange("(c b) s e -> c s b e", b=NB)
    cv = ctx.rearrange("(c b) s e -> c s b e", b=NB)
    ov = out.rearrange("(c b) s e -> c s b e", b=NB)

    ORDER = []
    for c in range(NCH):
        for w, (n, first, apart) in PLACE.items():
            ORDER += [(CHUNK_AT[c] + first + apart * t, c, w, t) for t in range(n)]
    ORDER = [s[1:] for s in sorted(ORDER)]
    F_USES = [s for s in ORDER if s[1] in F_STEPS]
    S_USES = [s for s in ORDER if s[1] in S_STEPS]
    F_USE = {s: n for n, s in enumerate(F_USES)}
    S_USE = {s: n for n, s in enumerate(S_USES)}
    TR_LAST = {"xT": "v", "cT": "cv", "x1T": "cq", "XT": "o", "cXT": "co"}
    TR_USES = [s for s in ORDER if s[1] in TR_LAST]
    OT_USES = [s for s in ORDER if s[1] in ("pv", "cpv")]

    st = ExitStack()
    with st:
        def sb(name, shape, dt=F32):
            return st.enter_context(nc.sbuf_tensor(name, shape, dt))

        def sem(name):
            return st.enter_context(nc.semaphore(name))

        ident = sb("ident", [P, P])
        identb = sb("identb", [P, P], BF16)
        maskT = sb("maskT", [P, 1, S], BF16)
        wT = sb("wT", [P, 8, P])
        bcol = sb("bcol", [P, NQ])
        brow = sb("brow", [P, 4, E])
        rb_row = sb("rb_row", [P, NEXP])
        hb = sb("hb", [P, NEXP + 1, NF])
        ob = sb("ob", [NEXP + 1, E])
        w1 = sb("w1", [P, NEXP + 1, HID])
        w2 = sb("w2", [P, NEXP + 1, NF, E])
        wr = sb("wr", [P, NEXP])
        tri = sb("tri", [P, NEXP, NEXP])
        epst = sb("epst", [P, NB])
        halfm = sb("halfm", [P, NB])
        RK = sb("RK", [KZ, WPAD], BF16)
        RV = sb("RV", [P, QD, NQ, HD])

        xin = [sb(f"xin{i}", [P, NB, E]) for i in range(2)]
        cin = sb("cin", [P, NB, E])
        TR = [sb(f"TR{i}", [P, T]) for i in range(2)]
        x2T = sb("x2T", [P, T])
        part = [sb(f"part{i}", [P, 3, T], BF16) for i in range(3)]
        rest = [sb(f"rest{i}", [P, T]) for i in range(2)]
        QS = [sb(f"QS{i}", [KD2, HB * S], BF16) for i in range(2)]
        KS = [sb(f"KS{i}", [KD2, HB * S], BF16) for i in range(2)]
        VA = [sb(f"VA{i}", [P, NB, H, HD + 1]) for i in range(2)]
        ST = sb("ST", [P, HB * S])
        PC = sb("PC", [P, NPC, TILE])
        MX = [sb(f"MX{i}", [P, HB * NQ]) for i in range(2)]
        NM = [sb(f"NM{i}", [P, 2, QD]) for i in range(2)]
        NR = [sb(f"NR{i}", [P, 2, QD]) for i in range(2)]
        MP = [sb(f"MP{i}", [P, NSH, 2, QD], BF16) for i in range(2)]
        OT = sb("OT", [P, 2 * BANK])
        OW = sb("OW", [P, H * S])
        X = [sb(f"X{i}", [P, NB, H, HD + 1]) for i in range(2)]
        Y = sb("Y", [P, NB, E])
        acc = sb("acc", [P, NB, E])
        stats = [sb(f"stats{i}", [P, NB, 6]) for i in range(3)]
        mv = [sb(f"mv{i}", [P, NB, 2]) for i in range(3)]
        ve = [sb(f"ve{i}", [P, NB]) for i in range(3)]
        rstd = [sb(f"rstd{i}", [P, NB]) for i in range(3)]
        x1 = sb("x1", [P, NB, E])
        x2 = sb("x2", [P, NB, E])
        lg = sb("lg", [P, NB, NEXP])
        lmax = sb("lmax", [P, NB])
        prob = sb("prob", [P, NB, NEXP])
        lsum = sb("lsum", [P, NB])
        gw = sb("gw", [P, NB, QD])
        gwT = sb("gwT", [NEXP + 1, NB, P])
        HT = [sb(f"HT{i}", [P, NF, T]) for i in range(2)]
        wnat = OT[:, 0:8 * P].rearrange("p (w i) -> p w i", w=8)
        relx = OW[0:HD, 0:WPAD]
        relr = OW[0:HD, WPAD:2 * WPAD]
        relp = OW[0:HD, 2 * WPAD:2 * WPAD + 3 * WPAD // 2].bitcast(BF16).rearrange("d (p w) -> d p w", p=3)
        brows = OW[0:NQ, 4 * WPAD:4 * WPAD + E]
        rv_nat = PC[:, 0, :].rearrange("p (a j d) -> p a j d", a=NQ, j=QD)
        cmp_, cmp2 = (Y[:, 2 * i:2 * i + 2, :].rearrange("p b (r e j) -> p (b r) e j", e=NEXP, j=NEXP) for i in range(2))
        rank = sb("rank", [P, NB, NEXP])

        ps_s = [st.enter_context(nc.psum_tensor(f"ps_s{i}", [P, TILE], F32)) for i in range(2)]
        ps_f = [st.enter_context(nc.psum_tensor(f"ps_f{i}", [P, BANK], F32)) for i in range(4)]

        ld_w = [sem(f"ld_w{i}") for i in range(2)]
        ld_b = sem("ld_b")
        ld_br = sem("ld_br")
        ld_e = sem("ld_e")
        ld_rel = sem("ld_rel")
        ext_done = sem("ext_done")
        ld_rk = sem("ld_rk")
        ld_rv = sem("ld_rv")
        rv_ready = sem("rv_ready")
        ld_x = sem("ld_x")
        ld_c = sem("ld_c")
        c_pool = sem("c_pool")
        zeroed = [sem(f"zeroed{i}") for i in range(2)]
        ones = sem("ones")
        rk_zero = sem("rk_zero")
        c_dve = sem("c_dve")
        rel_step = sem("rel_step")
        wt_ps = sem("wt_ps")
        wt_sb = sem("wt_sb")
        spread_out = {k: sem(f"spread_out_{k}") for k in ("q", "k", "ck", "cq")}
        s_full = sem("s_full")
        f_full = sem("f_full")
        T_ready = {k: sem(f"{k}_ready") for k in ("xT", "x1T", "x2T", "cT", "XT", "cXT")}
        hi_ready = {k: sem(f"hi_{k}") for k in ("q", "k", "ck", "cq")}
        rest_ready = {k: sem(f"rest_{k}") for k in ("q", "k", "ck", "cq")}
        mid_ready = {k: sem(f"mid_{k}") for k in ("q", "k", "ck", "cq")}
        low_ready = {k: sem(f"low_{k}") for k in ("q", "k", "ck", "cq")}
        stacked = {k: sem(f"stacked_{k}") for k in ("q", "k", "ck", "cq")}
        va_ready = [sem(f"va_ready{i}") for i in range(2)]
        bias_ready = sem("bias_ready")
        sum_ready = sem("sum_ready")
        mx_ready = [sem(f"mx_ready{i}") for i in range(2)]
        negmax = [sem(f"negmax{i}") for i in range(2)]
        mp_step = [sem(f"mp_step{i}") for i in range(2)]
        shifted = [[sem(f"shifted{i}_{f}") for f in range(2)] for i in range(2)]
        sc_ready = sem("sc_ready")
        ex_ready = sem("ex_ready")
        pr_ready = [sem(f"pr_ready{i}") for i in range(2)]
        ot_ready = [sem(f"ot_ready{i}") for i in range(2)]
        ow_ready = sem("ow_ready")
        xu_ready = [sem(f"xu_ready{i}") for i in range(2)]
        xw_ready = sem("xw_ready")
        rl_ready = [sem(f"rl_ready{i}") for i in range(2)]
        X_ready = [sem(f"X_ready{i}") for i in range(2)]
        res_ready = [sem(f"res_ready{i}") for i in range(2)]
        y_ready = [sem(f"y_ready{i}") for i in range(2)]
        st_ready = [sem(f"st_ready{i}") for i in range(3)]
        mv_ready = [sem(f"mv_ready{i}") for i in range(3)]
        ve_ready = [sem(f"ve_ready{i}") for i in range(3)]
        rstd_ready = [sem(f"rstd_ready{i}") for i in range(3)]
        ln_ready = [sem(f"ln_ready{i}") for i in range(3)]
        r_step = sem("r_step")
        lg_ready = sem("lg_ready")
        exp_ready = sem("exp_ready")
        gw_ready = sem("gw_ready")
        gwT_ready = sem("gwT_ready")
        ht_ready = sem("ht_ready")
        dn_done = sem("dn_done")
        stored = sem("stored")

        AB = {"q": 0, "k": 0, "ck": 1, "cq": 1}

        def released(s):
            ch, what, t = s
            return {
                "xT": lambda: (T_ready["xT"], ch + 1), "x1T": lambda: (T_ready["x1T"], ch + 1),
                "x2T": lambda: (T_ready["x2T"], ch + 1), "cT": lambda: (T_ready["cT"], ch + 1),
                "XT": lambda: (T_ready["XT"], ch + 1), "cXT": lambda: (T_ready["cXT"], ch + 1),
                "q": lambda: (rest_ready["q"], ch + 1), "k": lambda: (rest_ready["k"], ch + 1),
                "ck": lambda: (rest_ready["ck"], ch + 1), "cq": lambda: (rest_ready["cq"], ch + 1),
                "v": lambda: (va_ready[0], ch + 1), "cv": lambda: (va_ready[1], ch + 1),
                "m": lambda: (negmax[0], 2 * ch + t + 1), "cm": lambda: (negmax[1], 2 * ch + t + 1),
                "pv": lambda: (ot_ready[0], NQ * ch + t + 1), "cpv": lambda: (ot_ready[1], NQ * ch + t + 1),
                "w2": lambda: (ow_ready, NQ * ch + t + 1),
                "pvT": lambda: (xu_ready[0], NQ * ch + t + 1), "cpvT": lambda: (xu_ready[1], NQ * ch + t + 1),
                "w2T": lambda: (xw_ready, NQ * ch + t + 1),
                "o": lambda: (y_ready[0], ch + 1), "co": lambda: (y_ready[1], ch + 1),
                "r": lambda: (r_step, R_STEPS * ch + 1), "g": lambda: (gwT_ready, ch + 1),
                "dn": lambda: (dn_done, (NEXP + 1) * ch + t + 1),
                "bias": lambda: (bias_ready, NT * ch + t + 1), "p1": lambda: (mx_ready[0], NT * ch + t + 1),
                "p2": lambda: (sc_ready, NT * ch + t + 1), "c1": lambda: (mx_ready[1], NT * ch + t + 1),
                "c2": lambda: (ex_ready, NT * ch + t + 1), "up": lambda: (ht_ready, N_UP * ch + t + 1),
            }[what]()
        R_STEPS = 9
        N_UP = (NEXP + 1) * NF

        def bias_on_pe(ch, t):
            return ch == 0 and t % 2 == 1

        def take_f(pe, s):
            n = F_USE[s]
            if n >= 4:
                pe.wait_ge(*released(F_USES[n - 4]))
            return ps_f[n % 4]

        def take_s(pe, s):
            n = S_USE[s]
            if n >= 2:
                pe.wait_ge(*released(S_USES[n - 2]))
            return ps_s[n % 2]

        def done_f(e, s):
            e.wait_ge(f_full, F_USE[s] + 1)
            return ps_f[F_USE[s] % 4]

        def transposed(s):
            return TR[TR_USES.index(s) % 2]

        def ot_slot(s):
            return OT_USES.index(s) % 2 * BANK

        def done_s(e, s):
            e.wait_ge(s_full, S_USE[s] + 1)
            return ps_s[S_USE[s] % 2]

        block = st.enter_context(nc.Block())
        N_E = 10
        q_runs, k_runs = runs(Q_PART), runs(K_PART)
        N_RUNS = {"q": len(q_runs), "k": len(k_runs), "ck": len(k_runs), "cq": len(q_runs)}
        SLOT = {"q": 0, "k": 1, "ck": 2, "cq": 3}

        @block.sync
        def _(sp):
            def load_x(ch):
                if ch >= 2:
                    sp.wait_ge(y_ready[0], ch - 1)
                sp.dma_start(xin[ch % 2][:, :, :], xv[ch]).then_inc(ld_x, 16)

            def load_c(ch):
                if ch:
                    done_f(sp, (ch - 1, "cT", 0))
                sp.dma_start(cin[:, :, :], cv[ch]).then_inc(ld_c, 16)

            load_x(0)
            for i in range(2):
                sp.dma_start(wnat[:, i, :], sw[i][0]).then_inc(ld_w[0], 16)
            sp.dma_start(relx[:, S - 1 - MAX_REL:S + MAX_REL], rel_k.rearrange("r d -> d r"),
                         allow_slow_non_contiguous=True).then_inc(ld_rel, 16)
            for i, (w, _) in enumerate(cw):
                sp.dma_start(wnat[:, 4 + i, :], w).then_inc(ld_w[1], 16)
            for i, b in enumerate([sw[2][1], sw[3][1], cw[2][1], cw[3][1]]):
                sp.dma_start(brow[:, i, :], b.rearrange("(o e) -> o e", o=1).broadcast_to([P, E])).then_inc(ld_br, 16)
            load_c(0)
            sp.wait_ge(rel_step, 5)
            sp.wait_ge(rk_zero, 1)
            for c in range(NC):
                sp.dma_start(RK[c * HD:(c + 1) * HD, :], relp[:, K_PART[c], :]).then_inc(ld_rk, 16)

            def load_relative_values():
                n_end = S - 1 - MAX_REL
                sp.dma_start(rel_ext[n_end:S + MAX_REL, :], rel_v).then_inc(ext_done, 16)
                sp.dma_start(rel_ext[0:n_end, :], rel_v[0:1, :].broadcast_to([n_end, HD])).then_inc(ext_done, 16)
                sp.dma_start(rel_ext[S + MAX_REL:WIN, :],
                             rel_v[NREL - 1:NREL, :].broadcast_to([n_end, HD])).then_inc(ext_done, 16)
                sp.wait_ge(ext_done, 48)
                win = bass.AP(rel_ext.tensor, 0, [[HD, P], [HD, S], [1, HD]])
                sp.dma_start(rv_nat.rearrange("p a j d -> p (a j) d"), win).then_inc(ld_rv, 16)

            def load_experts():
                sp.dma_start(rb_row[:, :], router_b.rearrange("(o e) -> o e", o=1).broadcast_to([P, NEXP])).then_inc(ld_e, 16)
                sp.dma_start(hb[:, 0:NEXP, :], rb1.rearrange("e (f p) -> p e f", p=P),
                             allow_slow_non_contiguous=True).then_inc(ld_e, 16)
                sp.dma_start(hb[:, NEXP, :], sb1.rearrange("(f p) -> p f", p=P),
                             allow_slow_non_contiguous=True).then_inc(ld_e, 16)
                sp.dma_start(ob[0:NEXP, :], rb2).then_inc(ld_e, 16)
                sp.dma_start(ob[NEXP:NEXP + 1, :], sb2.rearrange("(o e) -> o e", o=1)).then_inc(ld_e, 16)
                sp.dma_start(w1[:, 0:NEXP, :], rw1.rearrange("e d h -> d e h")).then_inc(ld_e, 16)
                sp.dma_start(w1[:, NEXP, :], sw1).then_inc(ld_e, 16)
                sp.dma_start(w2[:, 0:NEXP, :, :].rearrange("p e f d -> p (e f) d"),
                             rw2.rearrange("e (f p) d -> p (e f) d", p=P)).then_inc(ld_e, 16)
                sp.dma_start(w2[:, NEXP, :, :], sw2.rearrange("(f p) d -> p f d", p=P)).then_inc(ld_e, 16)
                sp.dma_start(wr[:, :], router_w).then_inc(ld_e, 16)

            def spread_parts(ch, what):
                sp.wait_ge(low_ready[what], ch + 1)
                sp.dma_start(spread[4 * ch + SLOT[what]].rearrange("e p t -> p e t"),
                             part[min(SLOT[what], 2)][:, :, :]).then_inc(spread_out[what], 16)

            def stack(ch, what):
                a = AB[what]
                if ch == 0:
                    sp.wait_ge(zeroed[a], 2)
                sp.wait_ge(spread_out[what], 16 * (ch + 1))
                if ch:
                    done_s(sp, (ch - 1, "c2" if a else "p2", NT - 1))
                dst, rr = (QS[a], q_runs) if what in ("q", "cq") else (KS[a], k_runs)
                rows = spread[4 * ch + SLOT[what]].rearrange("e (d h) t -> (e d) (h t)", h=H)
                for c, p, n_ in rr:
                    sp.dma_start(dst[c * HD:(c + n_) * HD, :],
                                 rows[p * HD:(p + n_) * HD, :]).then_inc(stacked[what], 16)

            def shifts(ch, a, t):
                sp.wait_ge(mp_step[a], 4 * (2 * ch + t) + 4)
                for p in range(NSH):
                    dst = QS[a][KZ + p:KZ + p + 1, t * P * QD:(t + 1) * P * QD]
                    sp.dma_start(dst.rearrange("o (r i) -> o r i", i=QD), MP[a][:, p, t, :]).then_inc(shifted[a][t], 16)

            for ch, what, t in ORDER:
                if what == "xT" and ch + 1 < NCH:
                    load_x(ch + 1)
                elif what in SLOT:
                    spread_parts(ch, what)
                    if what == "k" and ch:
                        stack(ch, "q")
                    if what != "q" or ch == 0:
                        stack(ch, what)
                    if ch == 0 and what == "k":
                        load_relative_values()
                        load_experts()
                elif what == "cT" and ch + 1 < NCH:
                    load_c(ch + 1)
                elif what in ("m", "cm"):
                    shifts(ch, int(what == "cm"), t)
                elif what == "fln":
                    sp.wait_ge(ln_ready[2], ch + 1)
                    sp.dma_start(ov[ch], acc[:, :, :]).then_inc(stored, 16)
            sp.wait_ge(stored, 16 * NCH)

        @block.gpsimd
        def _(g):
            def zeros(a):
                nc.gpsimd.memset(QS[a][0:KD2, :].bitcast(F32), 0.0).then_inc(zeroed[a], 1)
                nc.gpsimd.memset(KS[a][0:KD2, :].bitcast(F32), 0.0).then_inc(zeroed[a], 1)

            nc.gpsimd.memset(ident[:, :], 0.0).then_inc(c_pool, 1)
            g.wait_ge(c_pool, 1)
            nc.gpsimd.affine_select(out=ident[:, :], in_=ident[:, :], compare_op=ALU.not_equal, fill=1.0,
                                    base=0, pattern=[[-1, P]], channel_multiplier=1).then_inc(c_pool, 1)
            nc.gpsimd.memset(RK[0:KZ, :], 0.0).then_inc(rk_zero, 1)
            zeros(0)
            nc.gpsimd.memset(tri[:, :, :], 1.0).then_inc(c_pool, 1)
            nc.gpsimd.memset(epst[:, :], EPS).then_inc(c_pool, 1)
            nc.gpsimd.memset(halfm[:, :], -0.5).then_inc(c_pool, 1)
            nc.gpsimd.memset(maskT[:, :, :], 0.0).then_inc(c_pool, 1)
            g.wait_ge(c_pool, 6)
            nc.gpsimd.affine_select(out=maskT[:, :, :], in_=maskT[:, :, :], compare_op=ALU.is_ge, fill=MASKED,
                                    base=0, pattern=[[0, 1], [1, S]], channel_multiplier=-1).then_inc(c_pool, 1)
            nc.gpsimd.affine_select(out=tri[:, :, :], in_=tri[:, :, :], compare_op=ALU.is_gt, fill=0.0,
                                    base=0, pattern=[[1, NEXP], [-1, NEXP]], channel_multiplier=0).then_inc(c_pool, 1)
            nc.gpsimd.tensor_copy(identb[:, :], ident[:, :]).then_inc(c_pool, 1)
            g.wait_ge(c_pool, 9)
            zeros(1)
            g.wait_ge(ld_br, 16 * 4)

            for ch, what, t in ORDER:
                if what in ("xT", "x1T"):
                    a = int(what == "x1T")
                    r = x1 if a else xin[ch % 2]
                    done_f(g, (ch, what, 0))
                    nc.gpsimd.tensor_tensor(r[:, :, :], r[:, :, :],
                                            brow[:, 2 * a + 1:2 * a + 2, :].broadcast_to([P, NB, E]),
                                            ALU.add).then_inc(res_ready[a], 1)
                elif what == "bias" and ch == 0 and t == 0:
                    g.wait_ge(ld_rv, 16)
                    nc.gpsimd.tensor_copy(RV[:, :, :, :], rv_nat.rearrange("p a j d -> p j a d")).then_inc(rv_ready, 1)
                elif what == "c2":
                    n = NT * ch + t
                    g.wait_ge(ex_ready, n + 1)
                    w = PC[:, n % NPC, :].rearrange("p (g q) -> p g q", q=S)
                    nc.gpsimd.affine_select(out=w, in_=w, compare_op=ALU.is_ge, fill=0.0, base=0,
                                            pattern=[[0, HB_TILE], [1, S]], channel_multiplier=-1).then_inc(pr_ready[1], 1)
                elif what in ("o", "co", "fln"):
                    k = ["o", "co", "fln"].index(what)
                    g.wait_ge(mv_ready[k], ch + 1)
                    nc.gpsimd.tensor_tensor(ve[k][:, :], mv[k][:, :, 1], epst[:, :], ALU.add).then_inc(ve_ready[k], 1)
                    g.wait_ge(ve_ready[k], ch + 1)
                    nc.gpsimd.tensor_tensor(rstd[k][:, :], ve[k][:, :], halfm[:, :], ALU.pow).then_inc(rstd_ready[k], 1)

        @block.tensor
        def _(pe):
            pe.wait_ge(c_pool, 2)

            def weights(a):
                pe.wait_ge(ld_w[a], 16 * 4)
                for i in range(4):
                    nc.tensor.transpose(ps_s[a][:, i * P:(i + 1) * P], wnat[:, 4 * a + i, :],
                                        ident[:, :]).then_inc(wt_ps, 1)

            weights(0)
            pe.wait_ge(ld_b, 16 * 4)
            nc.tensor.transpose(ps_f[3][:, 0:NQ], brows, ident[0:NQ, 0:NQ]).then_inc(wt_ps, 1)
            pe.wait_ge(c_dve, 5)

            def transposes(s, src):
                ps = take_f(pe, s)
                for b in range(NB):
                    last = nc.tensor.transpose(ps[:, b * S:(b + 1) * S], src(b), ident[:, :])
                last.then_inc(f_full, 1)

            def project(s, w, src):
                ps = take_f(pe, s)
                nc.tensor.matmul(ps[:, :], wT[:, w, :], src[:, :], start=True, stop=True).then_inc(f_full, 1)

            def rows(s, w, src):
                ps = take_f(pe, s)
                for b in range(NB):
                    last = nc.tensor.matmul(ps[:, b * E:(b + 1) * E], src[:, b * S:(b + 1) * S], wT[:, w, :],
                                            start=True, stop=True)
                last.then_inc(f_full, 1)

            def scores(s, a, kd, masked, biased=False):
                ps, t = take_s(pe, s), s[2]
                for half in range(2):
                    if biased:
                        w = ST[:, t * TILE + half * BANK:t * TILE + (half + 1) * BANK]
                        nc.tensor.matmul(ps[:, half * BANK:(half + 1) * BANK], ident[:, :], w, start=True, stop=False,
                                         skip_group_check=True)
                    if masked:
                        nc.tensor.matmul(ps[:, half * BANK:(half + 1) * BANK], identb[:, :],
                                         maskT[:, :, :].broadcast_to([P, 4, S]), start=True, stop=False,
                                         skip_group_check=True)
                    for j in range(4):
                        c = (t * HB_TILE + half * 4 + j) * S
                        o = (half * 4 + j) * S
                        last = nc.tensor.matmul(ps[:, o:o + S], KS[a][0:kd, c:c + S], QS[a][0:kd, c:c + S],
                                                start=not masked and not biased and j == 0, stop=j == 3, skip_group_check=True)
                last.then_inc(s_full, 1)

            def maxima(s, a):
                ch, _, t = s
                pe.wait_ge(mx_ready[a], NT * ch + NT // 2 * (t + 1))
                ps = take_f(pe, s)
                nc.tensor.transpose(ps[:, 0:P], MX[a][:, t * P:(t + 1) * P], ident[:, :]).then_inc(f_full, 1)

            def values(s, a, prob_of):
                ps = take_f(pe, s)
                for j in range(HQ):
                    for b in range(NB):
                        h = HQ * s[2] + j
                        last = nc.tensor.matmul(ps[b * QD:b * QD + HD + 1, j * S:(j + 1) * S], VA[a][:, b, h, :],
                                                prob_of(h, b), start=j == 0, stop=j == HQ - 1,
                                                tile_position=(0, b * QD), skip_group_check=True)
                last.then_inc(f_full, 1)

            def to_tokens(s, src):
                ps = take_f(pe, s)
                for j in range(HQ):
                    last = nc.tensor.transpose(ps[:, j * P:(j + 1) * P], src(HQ * s[2] + j), ident[:, :])
                last.then_inc(f_full, 1)

            qs_q = QS[0][0:KZ, :].rearrange("k (g q) -> k g q", q=S)
            st_q = ST[:, :].rearrange("p (h b a j) -> p h b a j", h=H, b=NB, a=NQ)
            st_h = ST[:, :].rearrange("p (h b q) -> p h b q", h=H, b=NB)
            pc_h = PC[:, :, :].rearrange("p t (g b q) -> p t g b q", b=NB, q=S)

            for s in ORDER:
                ch, what, t = s
                if what == "xT":
                    pe.wait_ge(ld_x, 16 * (ch + 1))
                    transposes(s, lambda b: xin[ch % 2][:, b, :])
                elif what == "cT":
                    pe.wait_ge(ld_c, 16 * (ch + 1))
                    transposes(s, lambda b: cin[:, b, :])
                elif what == "x1T":
                    pe.wait_ge(ln_ready[0], ch + 1)
                    transposes(s, lambda b: x1[:, b, :])
                elif what == "x2T":
                    pe.wait_ge(ln_ready[1], ch + 1)
                    transposes(s, lambda b: x2[:, b, :])
                elif what in ("q", "k", "v"):
                    if ch == 0:
                        pe.wait_ge(c_dve, 6)
                    pe.wait_ge(T_ready["xT"], ch + 1)
                    if what == "v":
                        rows(s, 2, transposed((ch, "xT", 0)))
                        if ch == 0:
                            weights(1)
                    else:
                        project(s, "qk".index(what), transposed((ch, "xT", 0)))
                elif what in ("ck", "cv"):
                    pe.wait_ge(T_ready["cT"], ch + 1)
                    if what == "ck":
                        project(s, 5, transposed((ch, "cT", 0)))
                    else:
                        rows(s, 6, transposed((ch, "cT", 0)))
                elif what == "cq":
                    pe.wait_ge(T_ready["x1T"], ch + 1)
                    project(s, 4, transposed((ch, "x1T", 0)))
                elif what == "bias":
                    if t == 0:
                        pe.wait_ge(wt_sb, 5)
                        pe.wait_ge(stacked["q"], 16 * N_RUNS["q"] * (ch + 1))
                        pe.wait_ge(ld_rk, 16 * NC)
                    ps = take_s(pe, s)
                    for j in range(S // NT):
                        q = t * (S // NT) + j
                        last = nc.tensor.matmul(ps[:, j * HB:(j + 1) * HB], RK[:, S - 1 - q:2 * S - 1 - q],
                                                qs_q[:, :, q], start=True, stop=True)
                    last.then_inc(s_full, 1)
                elif what == "p1":
                    if t == 0:
                        pe.wait_ge(ones, 1)
                        pe.wait_ge(stacked["k"], 16 * N_RUNS["k"] * (ch + 1))
                    if bias_on_pe(ch, t):
                        pe.wait_ge(bias_ready, NT * (ch + 1))
                    scores(s, 0, KZ, False, bias_on_pe(ch, t))
                elif what in ("m", "cm"):
                    maxima(s, int(what == "cm"))
                elif what == "p2":
                    if t % (NT // 2) == 0:
                        pe.wait_ge(shifted[0][t // (NT // 2)], 16 * NSH * (ch + 1))
                    scores(s, 0, KD2, False)
                elif what == "c1":
                    if t == 0:
                        pe.wait_ge(ones, 2)
                        pe.wait_ge(c_pool, 9)
                        pe.wait_ge(stacked["ck"], 16 * N_RUNS["ck"] * (ch + 1))
                        pe.wait_ge(stacked["cq"], 16 * N_RUNS["cq"] * (ch + 1))
                    scores(s, 1, KZ, True)
                elif what == "c2":
                    if t % (NT // 2) == 0:
                        pe.wait_ge(shifted[1][t // (NT // 2)], 16 * NSH * (ch + 1))
                    scores(s, 1, KD2, False)
                elif what in ("pv", "cpv"):
                    a = int(what == "cpv")
                    pe.wait_ge(va_ready[a], ch + 1)
                    pe.wait_ge(pr_ready[a], NT * ch + 2 * t + 2)
                    values(s, a, (lambda h, b: pc_h[:, (NT * ch + h // 2) % NPC, h % 2, b, :]) if a else (lambda h, b: st_h[:, h, b, :]))
                elif what == "w2":
                    pe.wait_ge(pr_ready[0], NT * (ch + 1))
                    if t == 0:
                        pe.wait_ge(rv_ready, 1)
                    ps = take_f(pe, s)
                    for jj in range(QD // NQ):
                        j = t * (QD // NQ) + jj
                        for b in range(NB):
                            last = nc.tensor.matmul(ps[b * QD:(b + 1) * QD, jj * HB:(jj + 1) * HB],
                                                    RV[:, QD - 1 - j, :, :].rearrange("p a d -> p (a d)"),
                                                    st_q[:, :, b, :, j].rearrange("p h a -> p a h"),
                                                    start=jj == 0, stop=jj == QD // NQ - 1,
                                                    tile_position=(0, b * QD), skip_group_check=True)
                    last.then_inc(f_full, 1)
                elif what in ("pvT", "cpvT"):
                    pe.wait_ge(ot_ready[int(what == "cpvT")], NQ * ch + t + 1)
                    o = ot_slot((ch, what[:-1], t))
                    to_tokens(s, lambda h: OT[:, o + h % HQ * S:o + (h % HQ + 1) * S])
                elif what == "w2T":
                    pe.wait_ge(ow_ready, NQ * (ch + 1))
                    to_tokens(s, lambda h: OW[:, h * S:(h + 1) * S])
                elif what in ("XT", "cXT"):
                    a = int(what == "cXT")
                    pe.wait_ge(X_ready[a], ch + 1)
                    transposes(s, lambda b: Y[:, b, :])
                elif what in ("o", "co"):
                    a = int(what == "co")
                    pe.wait_ge(T_ready["cXT" if a else "XT"], ch + 1)
                    rows(s, 4 * a + 3, transposed((ch, "cXT" if a else "XT", 0)))
                elif what == "r":
                    pe.wait_ge(T_ready["x2T"], ch + 1)
                    pe.wait_ge(ld_e, 16 * N_E)
                    ps = take_f(pe, s)
                    for b in range(NB):
                        last = nc.tensor.matmul(ps[:, b * NEXP:(b + 1) * NEXP], x2T[:, b * S:(b + 1) * S], wr[:, :],
                                                start=True, stop=True)
                    last.then_inc(f_full, 1)
                elif what == "g":
                    pe.wait_ge(gw_ready, ch + 1)
                    ps = take_f(pe, s)
                    for b in range(NB):
                        last = nc.tensor.transpose(ps[0:QD, b * S:(b + 1) * S], gw[:, b, :], ident[:, :])
                    last.then_inc(f_full, 1)
                elif what == "up":
                    e, f = (t // NF - 1) % (NEXP + 1), t % NF
                    ps = take_f(pe, s)
                    nc.tensor.matmul(ps[:, :], w1[:, e, f * P:(f + 1) * P], x2T[:, :],
                                     start=True, stop=True).then_inc(f_full, 1)
                elif what == "dn":
                    e = (t - 1) % (NEXP + 1)
                    n = ch * (NEXP + 1) + t
                    pe.wait_ge(ht_ready, NF * (n + 1))
                    if t == 0:
                        pe.wait_ge(gwT_ready, ch + 1)
                    ps = take_f(pe, s)
                    for b in range(NB):
                        for f in range(NF):
                            last = nc.tensor.matmul(ps[:, b * E:(b + 1) * E], HT[n % 2][:, f, b * S:(b + 1) * S],
                                                    w2[:, e, f, :], start=f == 0, stop=f == NF - 1 and t > 0)
                        if t == 0:
                            last = nc.tensor.matmul(ps[:, b * E:(b + 1) * E], gwT[:, b, :], ob[:, :],
                                                    start=False, stop=True)
                    last.then_inc(f_full, 1)

        @block.scalar
        def _(act):
            for i in range(2, 4):
                nc.scalar.dma_start(wnat[:, i, :], sw[i][0]).then_inc(ld_w[0], 16)
            for i, b in enumerate([sw[0][1], sw[1][1], cw[0][1], cw[1][1]]):
                nc.scalar.dma_start(brows[i:i + 1, :].rearrange("o (d h) -> o d h", h=H),
                                    b.rearrange("(o h d) -> o d h", o=1, h=H), allow_slow_non_contiguous=True).then_inc(ld_b, 16)

            def weights(a):
                act.wait_ge(wt_ps, 5 * a + 4)
                src = ps_s[a][:, 0:BANK].rearrange("p (w o) -> p w o", w=4)
                nc.scalar.copy(wT[:, 4 * a:4 * a + 2, :].rearrange("p w (d h) -> p w d h", h=H),
                               src[:, 0:2, :].rearrange("p w (h d) -> p w d h", h=H)).then_inc(wt_sb, 1)
                nc.scalar.copy(wT[:, 4 * a + 2:4 * a + 4, :], src[:, 2:4, :]).then_inc(wt_sb, 1)

            weights(0)
            act.wait_ge(wt_ps, 5)
            nc.scalar.copy(bcol[:, :], ps_f[3][:, 0:NQ]).then_inc(wt_sb, 1)
            act.wait_ge(wt_sb, 3)

            for s in ORDER:
                ch, what, t = s
                if what in ("xT", "x1T", "x2T", "cT", "XT", "cXT"):
                    dst = x2T if what == "x2T" else transposed(s)
                    ps = done_f(act, s)
                    if what == "x2T" and ch:
                        done_f(act, (ch - 1, "up", N_UP - 1))
                    if what != "x2T" and TR_USES.index(s) >= 2:
                        c_, w_, _ = TR_USES[TR_USES.index(s) - 2]
                        done_f(act, (c_, TR_LAST[w_], 0))
                    nc.scalar.copy(dst[:, :], ps[:, :]).then_inc(T_ready[what], 1)
                elif what in SLOT:
                    ps = done_f(act, s)
                    i = min(SLOT[what], 2)
                    if what == "cq":
                        act.wait_ge(stacked["ck"], 16 * N_RUNS["ck"] * (ch + 1))
                    elif ch:
                        k = {"q": "q", "k": "k", "ck": "cq"}[what]
                        act.wait_ge(stacked[k], 16 * N_RUNS[k] * ch)
                    b = ["q", "k", "cq", "ck"].index(what)
                    nc.scalar.activation(part[i][:, 0, :], ps[:, :], ACT.Identity, bias=bcol[:, b:b + 1]).then_inc(hi_ready[what], 1)
                    act.wait_ge(rest_ready[what], ch + 1)
                    nc.scalar.copy(part[i][:, 1, :], rest[int(what in ("k", "ck"))][:, :]).then_inc(mid_ready[what], 1)
                    if ch == 0 and what == "k":
                        weights(1)
                elif what == "bias":
                    ps = done_s(act, s)
                    if t == 0 and ch:
                        done_f(act, (ch - 1, "w2", NQ - 1))
                    nq = S // NT
                    dst = ST[:, :].rearrange("p (g q) -> p g q", q=S)[:, :, t * nq:(t + 1) * nq]
                    nc.scalar.copy(dst, ps[:, :].rearrange("p (q g) -> p g q", g=HB)).then_inc(bias_ready, 1)
                elif what == "p2":
                    act.wait_ge(sc_ready, NT * ch + t + 1)
                    w = ST[:, t * TILE:(t + 1) * TILE]
                    nc.scalar.activation(w, w, ACT.Exp, scale=SCALE).then_inc(pr_ready[0], 1)
                elif what == "c2":
                    ps = done_s(act, s)
                    n = NT * ch + t
                    if n == 0:
                        act.wait_ge(rv_ready, 1)
                    if n >= NPC:
                        c_, t_ = divmod(n - NPC, NT)
                        done_f(act, (c_, "cpv", t_ // 2))
                    nc.scalar.activation(PC[:, n % NPC, :], ps[:, :], ACT.Exp, scale=SCALE).then_inc(ex_ready, 1)
                elif what in ("pv", "cpv"):
                    ps = done_f(act, s)
                    n = OT_USES.index(s)
                    if n >= 2:
                        c_, w_, t_ = OT_USES[n - 2]
                        done_f(act, (c_, w_ + "T", t_))
                    o = ot_slot(s)
                    nc.scalar.copy(OT[:, o:o + BANK], ps[:, :]).then_inc(ot_ready[int(what == "cpv")], 1)
                elif what == "w2":
                    ps = done_f(act, s)
                    if ch:
                        done_f(act, (ch - 1, "w2T", NQ - 1))
                    nj = QD // NQ
                    nc.scalar.copy(OW[:, :].rearrange("p (h a j) -> p h a j", h=H, a=NQ)[:, :, :, t * nj:(t + 1) * nj],
                                   ps[:, :].rearrange("p (j a h) -> p h a j", j=nj, a=NQ)).then_inc(ow_ready, 1)
                elif what in ("pvT", "cpvT"):
                    a = int(what == "cpvT")
                    ps = done_f(act, s)
                    if ch:
                        act.wait_ge(X_ready[a], ch)
                    nc.scalar.copy(X[a][:, :, HQ * t:HQ * (t + 1), :].rearrange("p b h d -> p h b d"),
                                   ps[:, :].rearrange("p (h b d) -> p h b d", h=HQ, b=NB)[:, :, :, 0:HD + 1]
                                   ).then_inc(xu_ready[a], 1)
                elif what == "r":
                    act.wait_ge(lg_ready, ch + 1)
                    nc.scalar.activation(prob[:, :, :], lg[:, :, :], ACT.Exp).then_inc(exp_ready, 1)
                elif what == "up":
                    e, f = (t // NF - 1) % (NEXP + 1), t % NF
                    n = ch * (NEXP + 1) + t // NF
                    ps = done_f(act, s)
                    if n >= 2:
                        c_, t_ = divmod(n - 2, NEXP + 1)
                        done_f(act, (c_, "dn", t_))
                    nc.scalar.activation(HT[n % 2][:, f, :], ps[:, :], ACT.Gelu,
                                         bias=hb[:, e, f:f + 1]).then_inc(ht_ready, 1)

        @block.vector
        def _(v):
            def one_rows(a):
                v.wait_ge(zeroed[a], 2)
                nc.vector.memset(KS[a][64:KD2, :].bitcast(F32), TWO_ONES).then_inc(ones, 1)

            for a in range(2):
                nc.vector.memset(VA[a][:, :, :, HD:HD + 1], 1.0).then_inc(c_dve, 1)
            nc.vector.memset(gw[:, :, :], 0.0).then_inc(c_dve, 1)
            v.wait_ge(c_dve, 3)
            nc.vector.memset(gw[:, :, NEXP:NEXP + 1], 1.0).then_inc(c_dve, 1)
            for i in range(3):
                last = nc.vector.memset(ps_f[i][:, :], 0.0)
            last.then_inc(c_dve, 1)
            v.wait_ge(ld_rel, 16)
            n_end = S - 1 - MAX_REL
            nc.vector.tensor_copy(relx[:, 0:n_end], relx[:, n_end:n_end + 1].broadcast_to([HD, n_end]))
            nc.vector.tensor_copy(relx[:, S + MAX_REL:WPAD],
                                  relx[:, S + MAX_REL - 1:S + MAX_REL].broadcast_to([HD, WPAD - S - MAX_REL])).then_inc(rel_step, 1)
            v.wait_ge(rel_step, 1)
            nc.vector.tensor_copy(relp[:, 0, :], relx).then_inc(rel_step, 1)
            v.wait_ge(rel_step, 2)
            nc.vector.tensor_tensor(relr, relx, relp[:, 0, :], ALU.subtract).then_inc(rel_step, 1)
            v.wait_ge(rel_step, 3)
            nc.vector.tensor_copy(relp[:, 1, :], relr).then_inc(rel_step, 1)
            v.wait_ge(rel_step, 4)
            nc.vector.tensor_tensor(relp[:, 2, :], relr, relp[:, 1, :], ALU.subtract).then_inc(rel_step, 1)
            v.wait_ge(wt_sb, 3)
            nc.vector.memset(ps_f[3][:, :], 0.0).then_inc(c_dve, 1)
            v.wait_ge(ld_br, 16 * 4)

            def flat(a):
                return a[:, :, :].rearrange("p b e -> p (b e)")

            def statistics(k, ch, y):
                for b in range(NB):
                    last = nc.vector.bn_stats(stats[k][:, b, :], y[:, b, :])
                last.then_inc(st_ready[k], 1)
                v.wait_ge(st_ready[k], ch + 1)
                for b in range(NB):
                    last = nc.vector.bn_aggr(mv[k][:, b, :], stats[k][:, b, :])
                last.then_inc(mv_ready[k], 1)

            def normalise(k, ch, y, o):
                v.wait_ge(rstd_ready[k], ch + 1)
                for b in range(NB):
                    last = nc.vector.tensor_scalar(o[:, b, :], y[:, b, :], mv[k][:, b, 0:1], rstd[k][:, b:b + 1],
                                                   ALU.subtract, ALU.mult)
                last.then_inc(ln_ready[k], 1)

            for s in ORDER:
                ch, what, t = s
                if what in SLOT:
                    ps = done_f(v, s)
                    i = min(SLOT[what], 2)
                    v.wait_ge(hi_ready[what], ch + 1)
                    k = int(what in ("k", "ck"))
                    b = ["q", "k", "cq", "ck"].index(what)
                    nc.vector.scalar_tensor_tensor(rest[k][:, :], ps[:, :], bcol[:, b:b + 1], part[i][:, 0, :],
                                                   ALU.add, ALU.subtract).then_inc(rest_ready[what], 1)
                    v.wait_ge(mid_ready[what], ch + 1)
                    nc.vector.tensor_tensor(part[i][:, 2, :], rest[k][:, :], part[i][:, 1, :],
                                            ALU.subtract).then_inc(low_ready[what], 1)
                elif what in ("v", "cv"):
                    a = int(what == "cv")
                    ps = done_f(v, s)
                    if ch:
                        done_f(v, (ch - 1, "cpv" if a else "pv", NQ - 1))
                    nc.vector.tensor_tensor(VA[a][:, :, :, 0:HD],
                                            ps[:, :].rearrange("p (b h d) -> p b h d", b=NB, h=H),
                                            brow[:, 2 * a:2 * a + 1, :].rearrange("p o (h d) -> p o h d", h=H)
                                            .broadcast_to([P, NB, H, HD]), ALU.add).then_inc(va_ready[a], 1)
                elif what == "bias" and ch == 0 and t % (NT // 2) == 0:
                    one_rows(t // (NT // 2))
                elif what == "p1":
                    ps = done_s(v, s)
                    if t == 0:
                        v.wait_ge(bias_ready, NT * (ch + 1))
                    if not bias_on_pe(ch, t):
                        nc.vector.tensor_tensor(ps[:, :], ps[:, :], ST[:, t * TILE:(t + 1) * TILE],
                                                ALU.add).then_inc(sum_ready, 1)
                        v.wait_ge(sum_ready, sum(not bias_on_pe(c, i) for c in range(ch + 1) for i in range(NT)
                                                 if (c, i) <= (ch, t)))
                    nc.vector.tensor_reduce(MX[0][:, t * 32:(t + 1) * 32], ps[:, :].rearrange("p (c i) -> p c i", i=QD),
                                            AXIS.X, ALU.max, apply_transpose=True).then_inc(mx_ready[0], 1)
                elif what == "c1":
                    ps = done_s(v, s)
                    nc.vector.tensor_reduce(MX[1][:, t * 32:(t + 1) * 32], ps[:, :].rearrange("p (c i) -> p c i", i=QD),
                                            AXIS.X, ALU.max, apply_transpose=True).then_inc(mx_ready[1], 1)
                elif what in ("m", "cm"):
                    a = int(what == "cm")
                    ps = done_f(v, s)
                    n = 2 * ch + t
                    nc.vector.tensor_reduce(NM[a][:, t, :], ps[:, 0:P].rearrange("p (a i) -> p i a", a=NQ),
                                            AXIS.X, ALU.max, negate=True).then_inc(negmax[a], 1)
                    v.wait_ge(negmax[a], n + 1)
                    if ch:
                        v.wait_ge(shifted[a][t], 16 * NSH * ch)
                    nc.vector.tensor_copy(MP[a][:, 0, t, :], NM[a][:, t, :]).then_inc(mp_step[a], 1)
                    v.wait_ge(mp_step[a], 4 * n + 1)
                    nc.vector.tensor_tensor(NR[a][:, t, :], NM[a][:, t, :], MP[a][:, 0, t, :], ALU.subtract).then_inc(mp_step[a], 1)
                    v.wait_ge(mp_step[a], 4 * n + 2)
                    nc.vector.tensor_copy(MP[a][:, 1, t, :], NR[a][:, t, :]).then_inc(mp_step[a], 1)
                    v.wait_ge(mp_step[a], 4 * n + 3)
                    nc.vector.tensor_tensor(MP[a][:, 2, t, :], NR[a][:, t, :], MP[a][:, 1, t, :], ALU.subtract).then_inc(mp_step[a], 1)
                elif what == "p2":
                    ps = done_s(v, s)
                    w = ST[:, t * TILE:(t + 1) * TILE]
                    nc.vector.tensor_tensor(w, ps[:, :], w, ALU.add).then_inc(sc_ready, 1)
                elif what == "w2T":
                    ps = done_f(v, s)
                    v.wait_ge(xu_ready[0], NQ * (ch + 1))
                    o = ps[:, :].rearrange("p (h b a d) -> p h b a d", h=HQ, b=NB, a=NQ)
                    for a in range(NQ):
                        r = slice(a * QD, (a + 1) * QD)
                        xo = X[0][r, :, HQ * t:HQ * (t + 1), 0:HD].rearrange("p b h d -> p h b d")
                        last = nc.vector.tensor_tensor(xo, o[r, :, :, NQ - 1 - a, :], xo, ALU.add)
                    last.then_inc(xw_ready, 1)
                elif what in ("X", "cX"):
                    a = int(what == "cX")
                    v.wait_ge(xu_ready[a], NQ * (ch + 1))
                    if not a:
                        v.wait_ge(xw_ready, NQ * (ch + 1))
                    den = X[a][:, :, :, HD:HD + 1]
                    nc.vector.reciprocal(den, den).then_inc(rl_ready[a], 1)
                    v.wait_ge(rl_ready[a], ch + 1)
                    nc.vector.tensor_tensor(Y[:, :, :].rearrange("p b (h d) -> p b h d", h=H), X[a][:, :, :, 0:HD], den.broadcast_to([P, NB, H, HD]), ALU.mult).then_inc(X_ready[a], 1)
                elif what in ("o", "co"):
                    a = int(what == "co")
                    ps = done_f(v, s)
                    v.wait_ge(res_ready[a], ch + 1)
                    nc.vector.tensor_tensor(flat(Y), ps[:, :], flat(x1 if a else xin[ch % 2]), ALU.add).then_inc(y_ready[a], 1)
                    v.wait_ge(y_ready[a], ch + 1)
                    statistics(a, ch, Y)
                elif what == "ln":
                    normalise(0, ch, Y, x1)
                elif what == "cln":
                    normalise(1, ch, Y, x2)
                elif what == "r":
                    ps = done_f(v, s)
                    if ch == 0:
                        v.wait_ge(ld_e, 16 * N_E)
                        v.wait_ge(c_pool, 9)
                    nc.vector.tensor_tensor(lg[:, :, :], ps[:, 0:NB * NEXP].rearrange("p (b e) -> p b e", b=NB),
                                            rb_row[:, :].rearrange("p (o e) -> p o e", o=1).broadcast_to([P, NB, NEXP]),
                                            ALU.add).then_inc(r_step, 1)
                    r = R_STEPS * ch
                    v.wait_ge(r_step, r + 1)
                    nc.vector.tensor_reduce(lmax[:, :], lg[:, :, :], AXIS.X, ALU.max).then_inc(r_step, 1)
                    v.wait_ge(r_step, r + 2)

                    def over(a):
                        return a[:, :].rearrange("p (b o) -> p b o", o=1).broadcast_to([P, NB, NEXP])
                    nc.vector.tensor_tensor(lg[:, :, :], lg[:, :, :], over(lmax), ALU.subtract).then_inc(lg_ready, 1)
                    v.wait_ge(exp_ready, ch + 1)
                    nc.vector.tensor_reduce(lsum[:, :], prob[:, :, :], AXIS.X, ALU.add).then_inc(r_step, 1)
                    v.wait_ge(r_step, r + 3)
                    nc.vector.reciprocal(lmax[:, :], lsum[:, :]).then_inc(r_step, 1)
                    v.wait_ge(r_step, r + 4)
                    nc.vector.tensor_tensor(prob[:, :, :], prob[:, :, :], over(lmax), ALU.mult).then_inc(r_step, 1)
                    v.wait_ge(r_step, r + 5)
                    pj = prob[:, :, :].rearrange("p b (o j) -> p b o j", o=1).broadcast_to([P, NB, NEXP, NEXP])
                    pi = prob[:, :, :].rearrange("p b (e o) -> p b e o", o=1).broadcast_to([P, NB, NEXP, NEXP])
                    nc.vector.tensor_tensor(cmp_[:, :, :, :], pj, pi, ALU.is_gt)
                    nc.vector.tensor_tensor(cmp2[:, :, :, :], pj, pi, ALU.is_equal).then_inc(r_step, 1)
                    v.wait_ge(r_step, r + 6)
                    tb = tri[:, :, :].rearrange("p (o e) j -> p o e j", o=1).broadcast_to([P, NB, NEXP, NEXP])
                    nc.vector.tensor_tensor(cmp2[:, :, :, :], cmp2[:, :, :, :], tb, ALU.mult).then_inc(r_step, 1)
                    v.wait_ge(r_step, r + 7)
                    nc.vector.tensor_tensor(cmp_[:, :, :, :], cmp_[:, :, :, :], cmp2[:, :, :, :], ALU.add).then_inc(r_step, 1)
                    v.wait_ge(r_step, r + 8)
                    nc.vector.tensor_reduce(rank[:, :, :], cmp_[:, :, :, :], AXIS.X, ALU.add).then_inc(r_step, 1)
                    v.wait_ge(r_step, r + 9)
                    nc.vector.scalar_tensor_tensor(gw[:, :, 0:NEXP], rank[:, :, :], float(TOP_K), prob[:, :, :],
                                                   ALU.is_lt, ALU.mult).then_inc(gw_ready, 1)
                elif what == "g":
                    ps = done_f(v, s)
                    nc.vector.tensor_copy(gwT[:, :, :].rearrange("p b t -> p (b t)"), ps[0:NEXP + 1, :]).then_inc(gwT_ready, 1)
                elif what == "dn":
                    n = ch * (NEXP + 1) + t
                    ps = done_f(v, s)
                    if t == 0:
                        if ch:
                            v.wait_ge(stored, 16 * ch)
                        nc.vector.tensor_tensor(flat(acc), ps[:, :], flat(x2), ALU.add).then_inc(dn_done, 1)
                    else:
                        v.wait_ge(dn_done, n)
                        for b in range(NB):
                            last = nc.vector.scalar_tensor_tensor(acc[:, b, :], ps[:, b * E:(b + 1) * E],
                                                                  gw[:, b, t - 1:t], acc[:, b, :], ALU.mult, ALU.add)
                        last.then_inc(dn_done, 1)
                elif what == "fln":
                    v.wait_ge(dn_done, (ch + 1) * (NEXP + 1))
                    statistics(2, ch, acc)
                    normalise(2, ch, acc, acc)


_ATTN = ["Wq", "bq", "Wk", "bk", "Wv", "bv", "Wo", "bo"]
_INS = (["x", "ctx_1024"] + [f"L0_attn_{n}" for n in _ATTN] + ["L0_attn_rel_k", "L0_attn_rel_v"]
        + [f"L0_xattn_{n}" for n in _ATTN]
        + [f"L0_ffn_{n}" for n in ["router_w", "router_b", "sw1", "sb1", "sw2", "sb2", "rw1", "rb1", "rw2", "rb2"]])


def kernel(**inputs):
    import numpy as np
    import concourse.bacc as bacc
    from concourse.bass_utils import run_bass_kernel_spmd as run

    nc = bacc.Bacc("TRN2", target_bir_lowering=False, num_devices=1)
    arrays, ap = {}, {}
    for name in _INS:
        a = np.ascontiguousarray(inputs[name])
        arrays[f"in_{name}"] = a
        ap[name] = nc.dram_tensor(f"in_{name}", a.shape, mybir.dt.from_np(a.dtype), kind="ExternalInput").ap()
    shape = inputs["x"].shape
    out = nc.dram_tensor("out_x", shape, mybir.dt.float32, kind="ExternalOutput").ap()
    rel_ext = nc.dram_tensor("rel_v_by_distance", (WIN, HD), mybir.dt.float32, kind="Internal").ap()
    spread = nc.dram_tensor("parts_by_head", (4 * (shape[0] // NB), 3, E, T), mybir.dt.bfloat16, kind="Internal").ap()

    def layer(p):
        return [(ap[f"{p}_W{n}"], ap[f"{p}_b{n}"]) for n in "qkvo"]
    f = {n[7:]: a for n, a in ap.items() if n.startswith("L0_ffn_")}
    build(nc, ap["x"], ap["ctx_1024"], layer("L0_attn"), layer("L0_xattn"), ap["L0_attn_rel_k"],
          ap["L0_attn_rel_v"], f["router_w"], f["router_b"], f["sw1"], f["sb1"], f["sw2"], f["sb2"],
          f["rw1"], f["rb1"], f["rw2"], f["rb2"], rel_ext, spread, out)
    r = run(nc, [arrays], core_ids=[0])
    return r.results[0]["out_x"]
```
